# Optimizing a Trainium2 kernel written in Bass

```python
import numpy as np
import jax
import jax.numpy as jnp

def _softmax(x, axis=-1):
    return jax.nn.softmax(x, axis=axis)

def _gelu(x):
    return jax.nn.gelu(x, approximate=True)

def _silu(x):
    return jax.nn.silu(x)

def _sigmoid(x):
    return jax.nn.sigmoid(x)

def _layernorm(x, axis=-1, eps=1e-05):
    m = jnp.mean(x, axis=axis, keepdims=True)
    v = jnp.var(x, axis=axis, keepdims=True)
    return (x - m) / jnp.sqrt(v + eps)

def _scatter_add(tgt, idx, src, axis=0):
    return tgt.at[idx].add(src)

def _segment_sum(src, seg, n):
    return jax.ops.segment_sum(src, seg, n)
kernel_name = 'mk_prb_d1_jaxref_r8_989fe9'

def setup_inputs(seed: int=0):
    np.random.seed(seed)
    _w = jnp.asarray

    def _L0_attn_setup():
        import jax, jax.numpy as jnp
        import numpy as np
        H = 16
        TOPK_RATIO = 0.05
        LN_EPS = 1e-05

        def _layernorm(t, gamma, beta):
            mu = t.mean(-1, keepdims=True)
            var = t.var(-1, keepdims=True)
            return (t - mu) * jax.lax.rsqrt(var + LN_EPS) * gamma + beta
        key = jax.random.key(seed)
        ks = jax.random.split(key, 4)
        B, N, C = (2, 256, 128)
        x = jax.random.normal(ks[0], (B, N, C), dtype=jnp.float32)
        Wqkv = jax.random.normal(ks[1], (3 * C, C), dtype=jnp.float32) * (1.0 / np.sqrt(C))
        Wproj = jax.random.normal(ks[2], (C, C), dtype=jnp.float32) * (1.0 / np.sqrt(C))
        return {'x': x, 'Wqkv': Wqkv, 'bqkv': jnp.zeros((3 * C,), jnp.float32), 'q_gamma': jnp.ones((C // H,), jnp.float32), 'q_beta': jnp.zeros((C // H,), jnp.float32), 'k_gamma': jnp.ones((C // H,), jnp.float32), 'k_beta': jnp.zeros((C // H,), jnp.float32), 'alpha': jnp.full((H,), 0.5, jnp.float32), 'Wproj': Wproj, 'bproj': jnp.zeros((C,), jnp.float32)}
    _L0_attn_in = _L0_attn_setup()

    def _L0_ffn_setup():
        import jax, jax.numpy as jnp
        import numpy as np
        NUM_OPS, B, T, D = (8, 8, 64, 128)
        key = jax.random.key(seed)
        k1, k2, k3, k4 = jax.random.split(key, 4)
        x = jax.random.normal(k1, (B, T, D), dtype=jnp.float32)
        W = jax.random.normal(k2, (NUM_OPS, D, D), dtype=jnp.float32) * 0.02
        b = jnp.zeros((NUM_OPS, D), dtype=jnp.float32)
        logits = 0.001 * jax.random.normal(k3, (NUM_OPS,), dtype=jnp.float32)
        u = jax.random.uniform(k4, (NUM_OPS,), dtype=jnp.float32, minval=1e-06, maxval=1.0 - 1e-06)
        return {'x': x, 'W': W, 'b': b, 'logits': logits, 'u': u}
    _L0_ffn_in = _L0_ffn_setup()
    _d = {'L0_attn_x': _L0_attn_in['x'], 'L0_attn_Wqkv': _L0_attn_in['Wqkv'], 'L0_attn_bqkv': _L0_attn_in['bqkv'], 'L0_attn_q_gamma': _L0_attn_in['q_gamma'], 'L0_attn_q_beta': _L0_attn_in['q_beta'], 'L0_attn_k_gamma': _L0_attn_in['k_gamma'], 'L0_attn_k_beta': _L0_attn_in['k_beta'], 'L0_attn_alpha': _L0_attn_in['alpha'], 'L0_attn_Wproj': _L0_attn_in['Wproj'], 'L0_attn_bproj': _L0_attn_in['bproj'], 'L0_ffn_W': _L0_ffn_in['W'], 'L0_ffn_b': _L0_ffn_in['b'], 'L0_ffn_logits': _L0_ffn_in['logits'], 'L0_ffn_u': _L0_ffn_in['u']}
    _x0 = _d['L0_attn_x']
    _d['L0_attn_x'] = jax.random.normal(jax.random.fold_in(jax.random.key(seed), 1), (32, 256, 128), dtype=_x0.dtype)
    del _x0
    return _d

def reference(L0_attn_x, L0_attn_Wqkv, L0_attn_bqkv, L0_attn_q_gamma, L0_attn_q_beta, L0_attn_k_gamma, L0_attn_k_beta, L0_attn_alpha, L0_attn_Wproj, L0_attn_bproj, L0_ffn_W, L0_ffn_b, L0_ffn_logits, L0_ffn_u):

    def _L0_attn_ref(x, Wqkv, bqkv, q_gamma, q_beta, k_gamma, k_beta, alpha, Wproj, bproj):
        import jax, jax.numpy as jnp
        import numpy as np
        H = 16
        TOPK_RATIO = 0.05
        LN_EPS = 1e-05

        def _layernorm(t, gamma, beta):
            mu = t.mean(-1, keepdims=True)
            var = t.var(-1, keepdims=True)
            return (t - mu) * jax.lax.rsqrt(var + LN_EPS) * gamma + beta
        B, N, C = x.shape
        D = C // H
        qkv = (x @ Wqkv.T + bqkv).reshape(B, N, 3, H, D).transpose(2, 0, 3, 1, 4)
        q, k, v = (qkv[0], qkv[1], qkv[2])
        q = _layernorm(q, q_gamma, q_beta)
        k = _layernorm(k, k_gamma, k_beta)
        scores = jnp.einsum('bhnd,bhmd->bhnm', q, k) / jnp.sqrt(jnp.float32(D))
        aw = jax.nn.softmax(scores, axis=-1)
        topk = max(1, int(N * TOPK_RATIO))
        kth = jax.lax.top_k(aw, topk)[0][..., -1:]
        mask = (aw >= kth).astype(aw.dtype)
        aws = aw * mask
        aws = aws / (aws.sum(-1, keepdims=True) + 1e-08)
        o_s = jnp.einsum('bhnm,bhmd->bhnd', aws, v)
        qf = jax.nn.softmax(q, axis=-1)
        kf = jax.nn.softmax(k, axis=-1)
        kv = jnp.einsum('bhnd,bhne->bhde', kf, v)
        z = jnp.einsum('bhnd,bhd->bhn', qf, kf.sum(axis=2))
        o_l = jnp.einsum('bhnd,bhde->bhne', qf, kv) / (z[..., None] + 1e-06)
        a = jax.nn.sigmoid(alpha).reshape(1, H, 1, 1)
        o = (a * o_s + (1.0 - a) * o_l).transpose(0, 2, 1, 3).reshape(B, N, C)
        return o @ Wproj.T + bproj

    def _L0_ffn_ref(x, W, b, logits, u):
        import jax, jax.numpy as jnp
        import numpy as np
        NUM_OPS, B, T, D = (8, 8, 64, 128)
        gumbel = -jnp.log(-jnp.log(u))
        idx = jnp.argmax(jax.nn.log_softmax(logits) + gumbel)
        out = jnp.einsum('btd,de->bte', x, W[idx]) + b[idx]
        return out
    x = L0_attn_x
    xn = _layernorm(x, axis=-1)
    x = x + _L0_attn_ref(xn, L0_attn_Wqkv, L0_attn_bqkv, L0_attn_q_gamma, L0_attn_q_beta, L0_attn_k_gamma, L0_attn_k_beta, L0_attn_alpha, L0_attn_Wproj, L0_attn_bproj) + _L0_ffn_ref(xn, L0_ffn_W, L0_ffn_b, L0_ffn_logits, L0_ffn_u)
    return x

_drawn_inputs = setup_inputs


def setup_inputs(seed=0):
    import zlib

    import numpy as np

    out = dict(_drawn_inputs(seed))
    spreads = {'L0_attn_bqkv': (0.0, 0.1),
     'L0_attn_q_gamma': (1.0, 0.2),
     'L0_attn_q_beta': (0.0, 0.1),
     'L0_attn_k_gamma': (1.0, 0.2),
     'L0_attn_k_beta': (0.0, 0.8),
     'L0_attn_alpha': (0.5, 0.6),
     'L0_attn_bproj': (0.0, 0.1),
     'L0_ffn_b': (0.0, 0.1)}
    factors = {}
    for name, (base, spread) in spreads.items():
        noise = np.random.default_rng([zlib.crc32(name.encode()), seed]).standard_normal(out[name].shape)
        drawn = base * np.exp(spread * noise) if base else spread * noise
        out[name] = jnp.asarray(drawn.astype(out[name].dtype))
    for name, factor in factors.items():
        out[name] = (out[name] * factor).astype(out[name].dtype)
    return out
```

```python
from contextlib import ExitStack

import numpy as np

import concourse.bass as bass
from concourse import mybir

F32 = mybir.dt.float32
BF16 = mybir.dt.bfloat16
ALU = mybir.AluOpType
ACT = mybir.ActivationFunctionType
AX_X = mybir.AxisListType.X

P = 128
H = 16
D = 8
C = H * D
N = 256
NT = N // P
TOPK = max(1, int(N * 0.05))
LN_EPS = 1e-5
SUM_EPS = 1e-8
Z_EPS = 1e-6
SCORE_SCALE = float(1.0 / np.sqrt(np.float32(D)))
UNITS = H // 2
TILES = 4
QUADS = H // 4
VW = 32
VA = D + 1
REMOVED = -1.0
HUGE = float(2 ** 40)
PARTS = 3
SLOTS = [(0, 0), (0, 1), (0, 2), (1, 0), (1, 1), (1, 2), (2, 0), (2, 1)]
ROWS = len(SLOTS) * D
POOL_TILES = 3


def wait(engine, semaphore, value):
    if isinstance(value, int) and value <= 0:
        return None
    return engine.wait_ge(semaphore, value)


def wait_alone(engine, semaphore, value, passed):
    w = wait(engine, semaphore, value)
    if w is not None:
        w.then_inc(passed, 1)


def build(nc, x, Wqkv, bqkv, q_gamma, q_beta, k_gamma, k_beta, alpha, Wproj, bproj, W, bW, logits, u, y):
    B = x.shape[0]
    OPS = W.shape[0]
    assert x.shape[1:] == (N, C) and 2 * ROWS == P

    scratch = nc.dram_tensor("part_slots", (2, H * ROWS, N), BF16, kind="Internal").ap()
    x_t = x.rearrange("b (t p) c -> b p t c", p=P)
    y_t = y.rearrange("b (t p) c -> b p t c", p=P)

    def exists(batch):
        return not isinstance(batch, int) or 0 <= batch < B

    with ExitStack() as ctx:
        def sb(name, shape, dt=F32):
            return ctx.enter_context(nc.sbuf_tensor(name, shape, dt))

        def ps(name, shape, dt=F32):
            return ctx.enter_context(nc.psum_tensor(name, shape, dt))

        def sem(name):
            return ctx.enter_context(nc.semaphore(name))

        ident = sb("ident", [P, P])
        minus_huge = sb("minus_huge", [P, P], BF16)
        own_head = sb("own_head", [P, H, VA])
        ones_row = sb("ones_row", [1, P])
        w_in = sb("w_in", [P, 4, P])
        w_qk = sb("w_qk", [P, 2 * C])
        w_v = sb("w_v", [P, C])
        w_proj = sb("w_proj", [P, C])
        w_mean = sb("w_mean", [P, 2 * H])
        b_row = sb("b_row", [1, 3 * C])
        b_mean = sb("b_mean", [1, 2 * H])
        b_out = sb("b_out", [1, C])
        w_ops = sb("w_ops", [P, OPS, C])
        b_ops = sb("b_ops", [1, OPS, C])
        w_sel = sb("w_sel", [P, C])
        b_sel = sb("b_sel", [1, C])
        gate = sb("gate", [P, 12, OPS])
        gamma_in = sb("gamma_in", [P, 2, D])
        beta_in = sb("beta_in", [P, 2, D])
        gamma = sb("gamma", [P, 2, H, D])
        beta = sb("beta", [P, 2, H, D])
        mix = sb("mix", [P, 4, H])

        x_sb = sb("x_sb", [P, 2, NT, C])
        stats = sb("stats", [P, NT, 6])
        x_mv = sb("x_mv", [P, NT, 2])
        x_ln = sb("x_ln", [P, NT])
        x_rstd = sb("x_rstd", [P, NT])
        xn = sb("xn", [P, NT, C])
        xnT = sb("xnT", [P, 2, N])
        qk_sq = sb("qk_sq", [P, NT * 2 * C])
        qk_raw = sb("qk_raw", [P, NT * 2 * C])
        qk_ss = sb("qk_ss", [P, NT * 2 * H])
        qk_ln = sb("qk_ln", [P, NT * 2 * H])
        qk_rstd = sb("qk_rstd", [P, NT * 2 * H])
        qk_a = sb("qk_a", [P, NT * 2 * C])
        qk_b = sb("qk_b", [P, NT * 2 * C])
        qkn = sb("qkn", [P, NT * 2 * C])
        qkT = sb("qkT", [P, 2, N])
        residue = sb("residue", [P, 2, 2, N])
        part = sb("part", [P, PARTS, 2, N], BF16)
        q_slots = sb("q_slots", [P, 2, UNITS, N], BF16)
        k_slots = sb("k_slots", [P, 2, UNITS, N], BF16)
        d_max = sb("d_max", [P, NT * 2 * H])
        d_sub = sb("d_sub", [P, NT * 2 * C])
        d_exp = sb("d_exp", [P, NT * 2 * C])
        d_sum = sb("d_sum", [P, NT * 2 * H])
        d_rec = sb("d_rec", [P, NT * 2 * H])
        feat = sb("feat", [P, NT, 2, C])
        v_aug = sb("v_aug", [P, 2, NT, H, VW])
        kv = sb("kv", [P, H, VA])
        qfT = sb("qfT", [P, N])
        lin_z = sb("lin_z", [P, 3, NT, H])
        lin = sb("lin", [P, 2, NT, C])
        ffn = sb("ffn", [P, NT, C])
        base = sb("base", [P, 2, NT, C])

        top8 = sb("top8", [P, 2, TILES, 8])
        drop8 = sb("drop8", [P, 2, TILES, 8])
        e8 = sb("e8", [P, 2, TILES, 8])
        next8 = sb("next8", [P, 4, TILES, 8])
        rest = sb("rest", [P, TILES, N])
        negmax = sb("negmax", [P, 2, TILES])
        e = sb("e", [P, 4, TILES, N])
        below = sb("below", [P, 4, TILES, N], BF16)
        kept = sb("kept", [P, 4, 2, NT, N])
        z = sb("z", [P, 2, NT, H])

        oT = sb("oT", [P, 2, QUADS, N])
        den = sb("den", [P, 3, NT, H])
        o_sparse = sb("o_sparse", [P, NT, C])
        o_sum = sb("o_sum", [P, NT, C])
        osT = sb("osT", [P, N])
        proj = sb("proj", [P, NT, C])
        out_sb = sb("out_sb", [P, NT, C])

        score_ps = ps("score_ps", [P, 2, 2, NT, N])
        turn_ps = ps("turn_ps", [P, 2, NT, N])
        pv_ps = ps("pv_ps", [P, 512])
        work_ps = ps("work_ps", [P, 512])

        names = """const_loaded w_loaded x_loaded y_stored pool_const pool_step setup_v setup_a setup_p gate_step
            scores_ready top_ready negmax_ready rest_ready next_ready drop_ready e8_ready waits_passed
            exp_done below_pool below_act turn_ready turn_copied pv_ready pv_copied
            x_stats x_mean x_logged x_rstd_ready xn_ready
            w_xT xT_copied w_qk_ready sq_ready raw_ready ss_ready qk_logged qk_rstd_ready
            n_step qkn_ready w_qkT qkT_copied part_ready residue_ready slots_written slots_loaded
            dmax_ready dsub_ready dexp_ready dsum_ready drec_ready feat_ready
            w_v_ready v_copied w_kv kv_ready w_qfT qfT_copied w_lin linz_step lin_ready
            w_ffn ffn_copied base_ready
            w_turn den_step osp_ready osum_ready w_osT osT_copied w_proj_ready proj_copied
            y_ready""".split()
        s = {n: sem(n) for n in names}

        block = ctx.enter_context(nc.Block())

        def iterations(engine, body):
            for it in (-2, -1, 0):
                body(it, it % 2)
            last = B - 4
            with engine.Fori(1, last, 2) as i:
                body(i, 1)
                body(i + 1, 0)
            for it in range(last + 1, B + 1):
                body(it, it % 2)
        assert B % 2 == 0 and B >= 6

        @block.sync
        def _(sp):
            for i, src in enumerate((Wqkv[0:P], Wqkv[P:2 * P], Wqkv[2 * P:3 * P], Wproj)):
                sp.dma_start(w_in[:, i, :], src).then_inc(s["w_loaded"], 16)
            for b in range(2):
                sp.dma_start(x_sb[:, b], x_t[b]).then_inc(s["x_loaded"], 16)
            sp.dma_start(b_row[:, :], bqkv.rearrange("(o c) -> o c", o=1)).then_inc(s["const_loaded"], 16)
            sp.dma_start(b_out[:, :], bproj.rearrange("(o c) -> o c", o=1)).then_inc(s["const_loaded"], 16)
            for i, (g_in, b_in) in enumerate(((q_gamma, q_beta), (k_gamma, k_beta))):
                sp.dma_start(gamma_in[:, i, :], g_in.partition_broadcast(P)).then_inc(s["const_loaded"], 16)
                sp.dma_start(beta_in[:, i, :], b_in.partition_broadcast(P)).then_inc(s["const_loaded"], 16)
            sp.dma_start(mix[:, 0, :], alpha.partition_broadcast(P)).then_inc(s["const_loaded"], 16)
            sp.dma_start(gate[:, 0, :], logits.partition_broadcast(P)).then_inc(s["const_loaded"], 16)
            sp.dma_start(gate[:, 1, :], u.partition_broadcast(P)).then_inc(s["const_loaded"], 16)
            sp.dma_start(w_ops[:, :, :], W.rearrange("o d e -> d o e")).then_inc(s["const_loaded"], 16)
            sp.dma_start(b_ops[:, :, :], bW.rearrange("(a o) e -> a o e", a=1)).then_inc(s["const_loaded"], 16)

            def body(it, par):
                nxt = 1 - par
                if exists(it + 2) and not (isinstance(it, int) and it < 0):
                    wait_alone(sp, s["base_ready"], it + 1, s["waits_passed"])
                    sp.dma_start(x_sb[:, par], x_t[it + 2]).then_inc(s["x_loaded"], 16)
                if exists(it + 1):
                    wait_alone(sp, s["slots_loaded"], 32 * (it + 1), s["waits_passed"])
                    for p in range(PARTS):
                        wait_alone(sp, s["part_ready"], PARTS * (it + 1) + p + 1, s["waits_passed"])
                        for slot, parts in enumerate(SLOTS):
                            for side in range(2):
                                if parts[side] == p:
                                    dst = scratch[side].rearrange("(h s d) n -> s h d n", h=H, d=D)[slot]
                                    sp.dma_start(dst, part[:, p, side, :]).then_inc(s["slots_written"], 16)
                    wait_alone(sp, s["slots_written"], 16 * 2 * len(SLOTS) * (it + 2), s["waits_passed"])
                    wait_alone(sp, s["scores_ready"], UNITS * it, s["waits_passed"])
                    for side, dst in enumerate((q_slots, k_slots)):
                        sp.dma_start(dst[:, nxt], scratch[side].rearrange("(g p) n -> p g n", p=P)).then_inc(
                            s["slots_loaded"], 16)
                if exists(it - 1):
                    wait_alone(sp, s["y_ready"], it, s["waits_passed"])
                    sp.dma_start(y_t[it - 1], out_sb[:]).then_inc(s["y_stored"], 16)

            iterations(sp, body)
            sp.wait_ge(s["y_stored"], 16 * B)

        @block.gpsimd
        def _(pool):
            def select(out, op, fill, base_, pattern, mult, n):
                pool.wait_ge(s["pool_step"], n)
                return nc.gpsimd.affine_select(out=out, in_=out, compare_op=op, fill=fill, base=base_,
                                               pattern=pattern, channel_multiplier=mult)
            nc.gpsimd.memset(ident[:], 0.0).then_inc(s["pool_step"], 1)
            nc.gpsimd.memset(minus_huge[:], 0.0).then_inc(s["pool_step"], 1)
            nc.gpsimd.memset(own_head[:], 1.0).then_inc(s["pool_step"], 1)
            nc.gpsimd.memset(ones_row[:], 1.0).then_inc(s["pool_const"], 1)
            nc.gpsimd.memset(v_aug[:], 0.0).then_inc(s["pool_step"], 1)
            select(ident[:], ALU.not_equal, 1.0, 0, [[-1, P]], 1, 4).then_inc(s["pool_const"], 1)
            select(minus_huge[:], ALU.not_equal, -HUGE, 0, [[-1, P]], 1, 4).then_inc(s["pool_const"], 1)
            select(own_head[:], ALU.is_ge, 0.0, 0, [[-D, H], [0, VA]], 1, 4).then_inc(s["pool_step"], 1)
            select(own_head[:], ALU.is_ge, 0.0, D - 1, [[D, H], [0, VA]], -1, 5).then_inc(s["pool_const"], 1)
            for par in range(2):
                nc.gpsimd.memset(v_aug[:, par, :, :, D:VA], 1.0).then_inc(s["pool_const"], 1)
            gb = gamma[:].rearrange("p a h d -> p (a h d)")
            bb = beta[:].rearrange("p a h d -> p (a h d)")

            def halves(ap):
                return ap.rearrange("p (t f) -> p t f", t=NT)

            def heads(ap):
                return ap.rearrange("p (g d) -> p g d", d=D)

            def spread(ap):
                return ap.unsqueeze(2).to_broadcast([P, NT * 2 * H, D])

            def body(it, par):
                nxt = 1 - par
                for u_ in range(UNITS):
                    g = it * UNITS + u_
                    if exists(it if u_ >= 2 else it - 1):
                        r = (u_ - 2) % 4
                        for t in range(POOL_TILES):
                            wait_alone(pool, s["next_ready"], TILES * (g - 2) + t + 1, s["waits_passed"])
                            nc.gpsimd.tensor_scalar(below[:, r, t, :], e[:, r, t, :],
                                                    next8[:, r, t, TOPK - 9:TOPK - 8], None,
                                                    ALU.is_lt).then_inc(s["below_pool"], 1)
                    if u_ == 0 and exists(it + 1):
                        pool.wait_ge(s["raw_ready"], it + 2)
                        pool.wait_ge(s["qk_rstd_ready"], it + 2)
                        nc.gpsimd.tensor_tensor(heads(qk_a[:]), heads(qk_raw[:]), spread(qk_rstd[:]),
                                                ALU.mult).then_inc(s["n_step"], 1)
                    if u_ == 1 and exists(it + 1):
                        pool.wait_ge(s["n_step"], 2 * (it + 1) + 1)
                        if isinstance(it, int) and it == -1:
                            pool.wait_ge(s["setup_v"], 1)
                        nc.gpsimd.tensor_tensor(halves(qk_b[:]), halves(qk_a[:]),
                                                gb.unsqueeze(1).to_broadcast([P, NT, 2 * C]),
                                                ALU.mult).then_inc(s["n_step"], 1)
                    if u_ == 1 and exists(it):
                        pool.wait_ge(s["ffn_copied"], it + 1)
                        wait(pool, s["y_ready"], it - 1)
                        nc.gpsimd.tensor_tensor(base[:, par], ffn[:], x_sb[:, par],
                                                ALU.add).then_inc(s["base_ready"], 1)
                    if u_ == 2 and exists(it + 1):
                        pool.wait_ge(s["n_step"], 2 * (it + 1) + 2)
                        nc.gpsimd.tensor_tensor(halves(qkn[:]), halves(qk_b[:]),
                                                bb.unsqueeze(1).to_broadcast([P, NT, 2 * C]),
                                                ALU.add).then_inc(s["qkn_ready"], 1)
                    if u_ == 3 and exists(it + 1):
                        pool.wait_ge(s["dmax_ready"], it + 2)
                        nc.gpsimd.tensor_tensor(heads(d_sub[:]), heads(qkn[:]), spread(d_max[:]),
                                                ALU.subtract).then_inc(s["dsub_ready"], 1)
                    if u_ in (3, 4) and exists(it + 1):
                        p = u_ - 3
                        pool.wait_ge(s["part_ready"], PARTS * (it + 1) + p + 1)
                        if p == 0:
                            pool.wait_ge(s["qkT_copied"], it + 2)
                        else:
                            pool.wait_ge(s["residue_ready"], 2 * (it + 1) + 1)
                        src = qkT[:] if p == 0 else residue[:, 0]
                        nc.gpsimd.tensor_tensor(residue[:, p], src, part[:, p],
                                                ALU.subtract).then_inc(s["residue_ready"], 1)
                    if u_ == 6 and exists(it - 1):
                        pool.wait_ge(s["osp_ready"], NT * it)
                        pool.wait_ge(s["lin_ready"], it)
                        nc.gpsimd.tensor_tensor(o_sum[:], o_sparse[:], lin[:, nxt],
                                                ALU.add).then_inc(s["osum_ready"], 1)
                    if u_ == 6 and exists(it + 1):
                        pool.wait_ge(s["drec_ready"], it + 2)
                        pool.wait_ge(s["dexp_ready"], 2 * (it + 2))
                        nc.gpsimd.tensor_tensor(heads(feat[:].rearrange("p t a c -> p (t a c)")), heads(d_exp[:]),
                                                spread(d_rec[:]), ALU.mult).then_inc(s["feat_ready"], 1)
                    if u_ == 7 and exists(it - 1):
                        pool.wait_ge(s["proj_copied"], it)
                        wait(pool, s["y_stored"], 16 * (it - 1))
                        nc.gpsimd.tensor_tensor(out_sb[:], proj[:], base[:, nxt], ALU.add).then_inc(s["y_ready"], 1)

            iterations(pool, body)

        @block.vector
        def _(dve):
            step = [0]

            def setup(ins):
                step[0] += 1
                ins.then_inc(s["setup_p"], 1)
                dve.wait_ge(s["setup_p"], step[0])

            dve.wait_ge(s["setup_a"], 1)
            wq4 = w_qk[:].rearrange("p (g d) -> p g d", d=D)
            setup(nc.vector.tensor_reduce(w_mean[:], wq4, AX_X, ALU.add))
            setup(nc.vector.tensor_scalar(w_mean[:], w_mean[:], 1.0 / D, None, ALU.mult))
            setup(nc.vector.tensor_tensor(wq4, wq4, w_mean[:].unsqueeze(2).to_broadcast([P, 2 * H, D]), ALU.subtract))
            dve.wait_ge(s["const_loaded"], 16 * 11)
            bq4 = b_row[:, 0:2 * C].rearrange("p (g d) -> p g d", d=D)
            setup(nc.vector.tensor_reduce(b_mean[:], bq4, AX_X, ALU.add))
            setup(nc.vector.tensor_scalar(b_mean[:], b_mean[:], 1.0 / D, None, ALU.mult))
            nc.vector.tensor_tensor(bq4, bq4, b_mean[:].unsqueeze(2).to_broadcast([1, 2 * H, D]),
                                    ALU.subtract).then_inc(s["setup_v"], 1)
            dve.wait_ge(s["setup_v"], 1)
            for i, factor in enumerate((SCORE_SCALE, 1.0)):
                for dst, src in ((gamma, gamma_in), (beta, beta_in)):
                    nc.vector.tensor_scalar(dst[:, i], src[:, i].unsqueeze(1).to_broadcast([P, H, D]), factor, None,
                                            ALU.mult).then_inc(s["setup_v"], 1)

            def stage_gate():
                setup(nc.vector.reduce_max(gate[:, 2, 0:1], gate[:, 0, :], AX_X))
                nc.vector.tensor_scalar(gate[:, 3, :], gate[:, 0, :], gate[:, 2, 0:1], None,
                                        ALU.subtract).then_inc(s["setup_v"], 1)
                for i in range(OPS):
                    last = nc.vector.memset(gate[:, 4, i:i + 1], float(OPS - i))
                setup(last)
                dve.wait_ge(s["setup_a"], 2)
                dve.wait_ge(s["setup_v"], 6)
                setup(nc.vector.tensor_scalar(gate[:, 3, :], gate[:, 3, :], gate[:, 5, 1:2], None, ALU.subtract))
                setup(nc.vector.tensor_tensor(gate[:, 3, :], gate[:, 3, :], gate[:, 6, :], ALU.subtract))
                setup(nc.vector.reduce_max(gate[:, 2, 1:2], gate[:, 3, :], AX_X))
                setup(nc.vector.scalar_tensor_tensor(out=gate[:, 7, :], in0=gate[:, 3, :], scalar=gate[:, 2, 1:2],
                                                     in1=gate[:, 4, :], op0=ALU.is_ge, op1=ALU.mult))
                setup(nc.vector.reduce_max(gate[:, 2, 2:3], gate[:, 7, :], AX_X))
                setup(nc.vector.tensor_scalar(gate[:, 8, :], gate[:, 7, :], gate[:, 2, 2:3], None, ALU.is_ge))
                for dst, src, one in ((w_sel, w_ops, gate), (b_sel, b_ops, gate[0:1])):
                    setup(nc.vector.tensor_scalar(dst[:], src[:, 0, :], one[:, 8, 0:1], None, ALU.mult))
                    for i in range(1, OPS):
                        setup(nc.vector.scalar_tensor_tensor(out=dst[:], in0=src[:, i, :], scalar=one[:, 8, i:i + 1],
                                                             in1=dst[:], op0=ALU.mult, op1=ALU.add))
                nc.vector.tensor_tensor(b_out[:], b_out[:], b_sel[:], ALU.add).then_inc(s["setup_v"], 1)
                setup(nc.vector.tensor_scalar(mix[:, 1, :], mix[:, 1, :], 1.0, None, ALU.add))
                setup(nc.vector.reciprocal(mix[:, 2, :], mix[:, 1, :]))
                setup(nc.vector.tensor_scalar(mix[:, 3, :], mix[:, 2, :], -1.0, 1.0, ALU.mult, ALU.add))

            def alone(semaphore, value):
                wait_alone(dve, semaphore, value, s["waits_passed"])

            def body(it, par):
                nxt = 1 - par

                def top(g, q, t):
                    alone(s["scores_ready"], g + 1)
                    nc.vector.max(top8[:, q, t, :], score_ps[:, q, t // 2, t % 2, :]).then_inc(s["top_ready"], 1)

                def remove(u_, t):
                    g1 = it * UNITS + u_ - 1
                    wait(dve, s["next_ready"], TILES * (g1 - 1) + t + 1)
                    alone(s["e8_ready"], g1 + 1)
                    nc.vector.match_replace(rest[:, t, :], e8[:, (u_ - 1) % 2, t, :], e[:, (u_ - 1) % 4, t, :],
                                            REMOVED).then_inc(s["rest_ready"], 1)

                def following(u_, t):
                    alone(s["rest_ready"], TILES * (it * UNITS + u_ - 1) + t + 1)
                    nc.vector.max(next8[:, (u_ - 1) % 4, t, :], rest[:, t, :]).then_inc(s["next_ready"], 1)

                def extra(u_, k):
                    if u_ == 0 and k == 0 and exists(it + 1):
                        dve.wait_ge(s["sq_ready"], it + 2)
                        nc.vector.tensor_reduce(qk_ss[:], qk_sq[:].rearrange("p (g d) -> p g d", d=D), AX_X,
                                                ALU.add).then_inc(s["ss_ready"], 1)
                    if u_ == 1 and k == 2 and exists(it):
                        dve.wait_ge(s["w_kv"], it + 1)
                        if isinstance(it, int) and it == 0:
                            dve.wait_ge(s["pool_const"], 6)
                        nc.vector.tensor_tensor(kv[:], work_ps[:, 0:H * VA].rearrange("p (h e) -> p h e", e=VA),
                                                own_head[:], ALU.mult).then_inc(s["kv_ready"], 1)
                    if u_ == 2 and 1 <= k <= 4 and exists(it):
                        w = work_ps[:, 0:NT * H * VA].rearrange("p (t h e) -> p t h e", t=NT, e=VA)
                        if k == 1:
                            dve.wait_ge(s["w_lin"], it + 1)
                            nc.vector.tensor_scalar(lin_z[:, 0], w[:, :, :, D], Z_EPS, None,
                                                    ALU.add).then_inc(s["linz_step"], 1)
                        if k == 2:
                            dve.wait_ge(s["linz_step"], 3 * it + 1)
                            nc.vector.reciprocal(lin_z[:, 1], lin_z[:, 0]).then_inc(s["linz_step"], 1)
                        if k == 3:
                            dve.wait_ge(s["linz_step"], 3 * it + 2)
                            nc.vector.tensor_tensor(lin_z[:, 2], lin_z[:, 1],
                                                    mix[:, 3, :].unsqueeze(1).to_broadcast([P, NT, H]),
                                                    ALU.mult).then_inc(s["linz_step"], 1)
                        if k == 4:
                            dve.wait_ge(s["linz_step"], 3 * it + 3)
                            nc.vector.tensor_tensor(
                                lin[:, par].rearrange("p t (h d) -> p (t h) d", d=D),
                                work_ps[:, 0:NT * H * VA].rearrange("p (g e) -> p g e", e=VA)[:, :, 0:D],
                                lin_z[:, 2].rearrange("p t h -> p (t h)").unsqueeze(2).to_broadcast([P, NT * H, D]),
                                ALU.mult).then_inc(s["lin_ready"], 1)
                    if u_ == 3 and k == 0 and exists(it + 1):
                        dve.wait_ge(s["qkn_ready"], it + 2)
                        nc.vector.tensor_reduce(d_max[:], qkn[:].rearrange("p (g d) -> p g d", d=D), AX_X,
                                                ALU.max).then_inc(s["dmax_ready"], 1)
                    if u_ in (4, 5) and 1 <= k <= 4 and exists(it - 1):
                        t = u_ - 4
                        w = work_ps[:].rearrange("p (h e) -> p h e", e=VW)
                        n = 3 * (NT * (it - 1) + t)
                        if k == 1:
                            dve.wait_ge(s["w_turn"], NT * (it - 1) + t + 1)
                            nc.vector.scalar_tensor_tensor(out=den[:, 0, t], in0=z[:, nxt, t], scalar=SUM_EPS,
                                                           in1=w[:, :, D], op0=ALU.mult,
                                                           op1=ALU.add).then_inc(s["den_step"], 1)
                        if k == 2:
                            dve.wait_ge(s["den_step"], n + 1)
                            nc.vector.reciprocal(den[:, 1, t], den[:, 0, t]).then_inc(s["den_step"], 1)
                        if k == 3:
                            dve.wait_ge(s["den_step"], n + 2)
                            nc.vector.tensor_tensor(den[:, 2, t], den[:, 1, t], mix[:, 2, :],
                                                    ALU.mult).then_inc(s["den_step"], 1)
                        if k == 4:
                            dve.wait_ge(s["den_step"], n + 3)
                            nc.vector.tensor_tensor(o_sparse[:, t].rearrange("p (h d) -> p h d", d=D), w[:, :, 0:D],
                                                    den[:, 2, t].unsqueeze(2).to_broadcast([P, H, D]),
                                                    ALU.mult).then_inc(s["osp_ready"], 1)
                    if u_ == 5 and exists(it + 2):
                        if k == 0:
                            dve.wait_ge(s["x_loaded"], 16 * (it + 3))
                            for t in range(NT):
                                nc.vector.bn_stats(stats[:, t], x_sb[:, par, t]).then_inc(s["x_stats"], 1)
                        if k == 2:
                            alone(s["x_stats"], NT * (it + 3))
                            for t in range(NT):
                                nc.vector.bn_aggr(x_mv[:, t], stats[:, t]).then_inc(s["x_mean"], 1)
                    if u_ == 5 and exists(it + 1):
                        if k == 5:
                            dve.wait_ge(s["dexp_ready"], 2 * (it + 2))
                            nc.vector.tensor_reduce(d_sum[:], d_exp[:].rearrange("p (g d) -> p g d", d=D), AX_X,
                                                    ALU.add).then_inc(s["dsum_ready"], 1)
                    if u_ == 6 and exists(it + 1) and k == 0:
                        dve.wait_ge(s["dsum_ready"], it + 2)
                        nc.vector.reciprocal(d_rec[:], d_sum[:]).then_inc(s["drec_ready"], 1)
                    if u_ == 6 and exists(it + 2) and k == 1:
                        dve.wait_ge(s["x_rstd_ready"], it + 3)
                        wait(dve, s["w_xT"], it + 3)
                        for t in range(NT):
                            nc.vector.tensor_scalar(xn[:, t], x_sb[:, par, t], x_mv[:, t, 0:1], x_rstd[:, t:t + 1],
                                                    ALU.subtract, ALU.mult).then_inc(s["xn_ready"], 1)

                if isinstance(it, int) and it == -1:
                    stage_gate()
                for u_ in range(UNITS):
                    g = it * UNITS + u_
                    q = u_ % 2
                    before = exists(it if u_ else it - 1)
                    if exists(it):
                        for t in range(TILES):
                            top(g, q, t)
                    if before:
                        remove(u_, 0)
                    if exists(it):
                        dve.wait_ge(s["top_ready"], TILES * (g + 1))
                        nc.vector.tensor_scalar(negmax[:, q, :], top8[:, q, :, 0], -1.0, None,
                                                ALU.mult).then_inc(s["negmax_ready"], 1)
                        nc.vector.tensor_tensor(drop8[:, q], top8[:, q], top8[:, q, :, 0:1].to_broadcast(
                            [P, TILES, 8]), ALU.subtract).then_inc(s["drop_ready"], 1)
                    extra(u_, 0)
                    if before:
                        remove(u_, 1)
                    extra(u_, 1)
                    if before:
                        following(u_, 0)
                    extra(u_, 2)
                    if before:
                        remove(u_, 2)
                    extra(u_, 3)
                    if before:
                        following(u_, 1)
                    extra(u_, 4)
                    if before:
                        remove(u_, 3)
                        following(u_, 2)
                    extra(u_, 5)
                    if before:
                        following(u_, 3)

            iterations(dve, body)

        @block.scalar
        def _(act):
            act.wait_ge(s["w_xT"], 1)
            nc.scalar.copy(w_qk[:], work_ps[:, 0:2 * C]).then_inc(s["setup_a"], 1)
            nc.scalar.copy(w_v[:], work_ps[:, 2 * C:3 * C])
            nc.scalar.copy(w_proj[:], work_ps[:, 3 * C:4 * C]).then_inc(s["xT_copied"], 1)

            def stage_gate():
                act.wait_ge(s["setup_v"], 6)
                nc.scalar.activation(gate[:, 9, :], gate[:, 3, :], ACT.Exp,
                                     accum_out=gate[:, 5, 0:1]).then_inc(s["gate_step"], 1)
                nc.scalar.activation(gate[:, 10, :], gate[:, 1, :], ACT.Ln).then_inc(s["gate_step"], 1)
                nc.scalar.activation(mix[:, 1, :], mix[:, 0, :], ACT.Exp, scale=-1.0).then_inc(s["gate_step"], 1)
                act.wait_ge(s["gate_step"], 3)
                nc.scalar.activation(gate[:, 5, 1:2], gate[:, 5, 0:1], ACT.Ln)
                nc.scalar.activation(gate[:, 6, :], gate[:, 10, :], ACT.Ln, scale=-1.0).then_inc(s["setup_a"], 1)

            def body(it, par):
                nxt = 1 - par
                if isinstance(it, int) and it == -1:
                    stage_gate()
                for u_ in range(UNITS):
                    g = it * UNITS + u_
                    if exists(it if u_ >= 2 else it - 1):
                        r = (u_ - 2) % 4
                        act.wait_ge(s["next_ready"], TILES * (g - 1))
                        for t in range(POOL_TILES, TILES):
                            nc.scalar.activation(below[:, r, t, :], e[:, r, t, :], ACT.Relu, scale=-1.0,
                                                 bias=next8[:, r, t, TOPK - 9:TOPK - 8]).then_inc(s["below_act"], 1)

                    if u_ == 0 and exists(it):
                        act.wait_ge(s["w_ffn"], it + 1)
                        wait(act, s["base_ready"], it)
                        nc.scalar.copy(ffn[:], work_ps[:, 0:NT * C].rearrange("p (t c) -> p t c", t=NT)).then_inc(
                            s["ffn_copied"], 1)
                    if u_ == 0 and exists(it + 1):
                        act.wait_ge(s["ss_ready"], it + 2)
                        nc.scalar.activation(qk_ln[:], qk_ss[:], ACT.Ln, scale=1.0 / D,
                                             bias=LN_EPS).then_inc(s["qk_logged"], 1)
                        act.wait_ge(s["qk_logged"], it + 2)
                        nc.scalar.activation(qk_rstd[:], qk_ln[:], ACT.Exp, scale=-0.5).then_inc(
                            s["qk_rstd_ready"], 1)
                    if u_ == 2 and exists(it):
                        act.wait_ge(s["w_qfT"], it + 1)
                        nc.scalar.copy(qfT[:], work_ps[:, 0:N]).then_inc(s["qfT_copied"], 1)
                    if u_ == 3 and exists(it + 1):
                        act.wait_ge(s["w_qkT"], it + 2)
                        wait(act, s["residue_ready"], 2 * (it + 1))
                        nc.scalar.copy(qkT[:], work_ps[:].rearrange("p (a n) -> p a n", a=2)).then_inc(
                            s["qkT_copied"], 1)
                        wait(act, s["slots_written"], 16 * 2 * len(SLOTS) * (it + 1))
                        nc.scalar.copy(part[:, 0], work_ps[:].rearrange("p (a n) -> p a n", a=2)).then_inc(
                            s["part_ready"], 1)
                    if u_ in (4, 5) and exists(it + 1):
                        p = u_ - 3
                        act.wait_ge(s["residue_ready"], 2 * (it + 1) + p)
                        nc.scalar.copy(part[:, p], residue[:, p - 1]).then_inc(s["part_ready"], 1)
                    if u_ == 4 and exists(it + 1):
                        act.wait_ge(s["w_v_ready"], it + 2)
                        nc.scalar.copy(v_aug[:, nxt, :, :, 0:D].rearrange("p t h d -> p (t h) d"),
                                       work_ps[:, 0:NT * C].rearrange("p (g d) -> p g d", d=D)).then_inc(
                                           s["v_copied"], 1)
                    if u_ == 5 and exists(it + 1):
                        act.wait_ge(s["dsub_ready"], it + 2)
                        sub = d_sub[:].rearrange("p (t a c) -> p t a c", t=NT, a=2)
                        dst = d_exp[:].rearrange("p (t a c) -> p t a c", t=NT, a=2)
                        for side, factor in enumerate((1.0 / SCORE_SCALE, 1.0)):
                            nc.scalar.activation(dst[:, :, side, :], sub[:, :, side, :], ACT.Exp,
                                                 scale=factor).then_inc(s["dexp_ready"], 1)
                    if u_ == 5 and exists(it + 2):
                        act.wait_ge(s["x_mean"], NT * (it + 3))
                        nc.scalar.activation(x_ln[:], x_mv[:, :, 1], ACT.Ln, bias=LN_EPS).then_inc(
                            s["x_logged"], 1)
                        act.wait_ge(s["x_logged"], it + 3)
                        nc.scalar.activation(x_rstd[:], x_ln[:], ACT.Exp, scale=-0.5).then_inc(
                            s["x_rstd_ready"], 1)
                    if u_ == 6 and exists(it + 2):
                        act.wait_ge(s["w_xT"], it + 4)
                        nc.scalar.copy(xnT[:, par], work_ps[:, 0:N]).then_inc(s["xT_copied"], 1)
                    if u_ == 7 and exists(it - 1):
                        act.wait_ge(s["w_osT"], it)
                        nc.scalar.copy(osT[:], work_ps[:, 0:N]).then_inc(s["osT_copied"], 1)
                    if u_ == 7 and exists(it + 2):
                        act.wait_ge(s["w_qk_ready"], it + 3)
                        nc.scalar.activation(qk_sq[:], work_ps[:], ACT.Square).then_inc(s["sq_ready"], 1)
                        wait(act, s["n_step"], 2 * (it + 2))
                        nc.scalar.copy(qk_raw[:], work_ps[:]).then_inc(s["raw_ready"], 1)

                    if exists(it if u_ >= 3 else it - 1):
                        wait(act, s["pv_ready"], it * QUADS + (u_ - 7) // 2 + 1)
                        for hh in range(2):
                            act.wait_ge(s["turn_ready"], 2 * (g - 3) + hh + 1)
                            nc.scalar.activation(kept[:, (u_ - 3) % 4, hh], turn_ps[:, hh], ACT.Relu).then_inc(
                                s["turn_copied"], 1)

                    if exists(it):
                        act.wait_ge(s["negmax_ready"], g + 1)
                        if u_ == 0:
                            wait(act, s["osp_ready"], NT * (it - 1))
                        wait(act, s["turn_ready"], 2 * (g - 3))
                        for t in range(TILES):
                            nc.scalar.activation(e[:, u_ % 4, t, :], score_ps[:, u_ % 2, t // 2, t % 2, :], ACT.Exp,
                                                 bias=negmax[:, u_ % 2, t:t + 1],
                                                 accum_out=z[:, par, t % 2, 2 * u_ + t // 2:2 * u_ + t // 2 + 1]
                                                 ).then_inc(s["exp_done"], 1)
                        act.wait_ge(s["drop_ready"], g + 1)
                        nc.scalar.activation(e8[:, u_ % 2], drop8[:, u_ % 2], ACT.Exp).then_inc(s["e8_ready"], 1)

                    quad = it * QUADS + (u_ - 5) // 2
                    if u_ % 2 == 1 and exists(it if u_ >= 5 else it - 1):
                        act.wait_ge(s["pv_ready"], quad + 1)
                        side = par if u_ >= 5 else nxt
                        if u_ == 5:
                            wait(act, s["w_turn"], NT * (it - 1))
                        nc.scalar.copy(oT[:, side, (u_ - 5) // 2 % 4], pv_ps[:, 0:N]).then_inc(
                            s["pv_copied"], 1)
                    if u_ == 7 and exists(it - 1):
                        act.wait_ge(s["w_proj_ready"], it)
                        wait(act, s["y_ready"], it - 1)
                        nc.scalar.copy(proj[:], work_ps[:, 0:NT * C].rearrange("p (t c) -> p t c", t=NT)).then_inc(
                            s["proj_copied"], 1)

            iterations(act, body)

        @block.tensor
        def _(pe):
            mm = nc.tensor.matmul
            pe.wait_ge(s["w_loaded"], 16 * 4)
            pe.wait_ge(s["pool_const"], 6)
            for i in range(4):
                last = nc.tensor.transpose(work_ps[:, i * P:(i + 1) * P], w_in[:, i, :], ident[:])
            last.then_inc(s["w_xT"], 1)

            def body(it, par):
                nxt = 1 - par

                def scores(u_):
                    g1 = it * UNITS + u_ + 1
                    side, v_ = (par, u_ + 1) if u_ < UNITS - 1 else (nxt, 0)
                    if v_ == 0:
                        pe.wait_ge(s["slots_loaded"], 32 * (it + 2))
                    wait_alone(pe, s["exp_done"], TILES * (g1 - 1), s["waits_passed"])
                    for t in range(TILES):
                        hh, nt = t // 2, t % 2
                        rows = slice(ROWS * hh, ROWS * (hh + 1))
                        last = mm(score_ps[:, v_ % 2, hh, nt, :], q_slots[rows, side, v_, nt * P:(nt + 1) * P],
                                  k_slots[rows, side, v_, :], start=True, stop=True)
                    last.then_inc(s["scores_ready"], 1)

                def turn(u_):
                    g2 = it * UNITS + u_ - 3
                    r = (u_ - 3) % 4
                    pe.wait_ge(s["below_pool"], POOL_TILES * (g2 + 1))
                    pe.wait_ge(s["below_act"], (TILES - POOL_TILES) * (g2 + 1))
                    for hh in range(2):
                        wait(pe, s["turn_copied"], 2 * (g2 - 1) + hh + 1)
                        for nt in range(NT):
                            t = 2 * hh + nt
                            for mc in range(NT):
                                dst = turn_ps[:, hh, mc, nt * P:(nt + 1) * P]
                                keys = slice(mc * P, (mc + 1) * P)
                                mm(dst, e[:, r, t, keys], ident[:], start=True, stop=False, is_transpose=True)
                                last = mm(dst, below[:, r, t, keys], minus_huge[:], start=False, stop=True)
                        last.then_inc(s["turn_ready"], 1)

                def product(u_):
                    quad = it * QUADS + (u_ - 5) // 2
                    side = par if u_ >= 5 else nxt
                    q = (u_ - 5) // 2 % 4
                    pe.wait_ge(s["turn_copied"], 4 * (quad + 1))
                    wait(pe, s["pv_copied"], quad)
                    for mc in range(NT):
                        for j in range(4):
                            v_ = 2 * q + j // 2
                            last = mm(pv_ps[32 * j:32 * (j + 1), 0:N], v_aug[:, side, mc, 4 * q + j, :],
                                      kept[:, v_ % 4, j % 2, mc, :], start=(mc == 0), stop=(mc == NT - 1),
                                      tile_position=(0, 32 * j))
                    last.then_inc(s["pv_ready"], 1)

                def jobs(u_):
                    if u_ == 0 and exists(it):
                        pe.wait_ge(s["raw_ready"], it + 1)
                        wait(pe, s["raw_ready"], it + 2 if exists(it + 1) else 0)
                        wait(pe, s["proj_copied"], it - 1)
                        pe.wait_ge(s["setup_v"], 7)
                        for t in range(NT):
                            dst = work_ps[:, t * C:(t + 1) * C]
                            mm(dst, xnT[:, par, t * P:(t + 1) * P], w_sel[:], start=True, stop=False)
                            last = mm(dst, ones_row[:], b_out[:], start=False, stop=True)
                        last.then_inc(s["w_ffn"], 1)
                    if u_ == 1 and exists(it):
                        pe.wait_ge(s["ffn_copied"], it + 1)
                        pe.wait_ge(s["feat_ready"], it + 1)
                        for t in range(NT):
                            last = mm(work_ps[:, 0:H * VA], feat[:, t, 1, :], v_aug[:, par, t, :, 0:VA],
                                      start=(t == 0), stop=(t == NT - 1))
                        last.then_inc(s["w_kv"], 1)
                    if u_ == 2 and exists(it):
                        pe.wait_ge(s["kv_ready"], it + 1)
                        for t in range(NT):
                            last = nc.tensor.transpose(work_ps[:, t * P:(t + 1) * P], feat[:, t, 0, :], ident[:])
                        last.then_inc(s["w_qfT"], 1)
                        pe.wait_ge(s["qfT_copied"], it + 1)
                        for t in range(NT):
                            last = mm(work_ps[:, t * H * VA:(t + 1) * H * VA], qfT[:, t * P:(t + 1) * P],
                                      kv[:].rearrange("p h e -> p (h e)"), start=True, stop=True)
                        last.then_inc(s["w_lin"], 1)
                    if u_ == 3:
                        if exists(it + 1):
                            wait(pe, s["lin_ready"], it + 1)
                            pe.wait_ge(s["qkn_ready"], it + 2)
                            for side in range(2):
                                for t in range(NT):
                                    last = nc.tensor.transpose(
                                        work_ps[:, side * N + t * P:side * N + (t + 1) * P],
                                        qkn[:, (2 * t + side) * C:(2 * t + side + 1) * C], ident[:])
                            last.then_inc(s["w_qkT"], 1)
                    if u_ == 4 and exists(it + 1):
                        wait(pe, s["part_ready"], PARTS * (it + 1) + 1)
                        for t in range(NT):
                            dst = work_ps[:, t * C:(t + 1) * C]
                            mm(dst, xnT[:, nxt, t * P:(t + 1) * P], w_v[:], start=True, stop=False)
                            last = mm(dst, ones_row[:], b_row[:, 2 * C:3 * C], start=False, stop=True)
                        last.then_inc(s["w_v_ready"], 1)
                    if u_ in (4, 5) and exists(it - 1):
                        t = u_ - 4
                        if t == 0:
                            pe.wait_ge(s["pv_copied"], QUADS * it)
                            wait(pe, s["lin_ready"], it + 1 if exists(it) else 0)
                            wait(pe, s["proj_copied"], 0 if exists(it) else it - 1)
                            wait(pe, s["v_copied"], it + 2 if exists(it + 1) else 0)
                        else:
                            pe.wait_ge(s["osp_ready"], NT * (it - 1) + 1)
                        for q in range(QUADS):
                            last = nc.tensor.transpose(work_ps[:, q * P:(q + 1) * P],
                                                       oT[:, nxt, q, t * P:(t + 1) * P], ident[:])
                        last.then_inc(s["w_turn"], 1)
                    if u_ == 6 and exists(it + 2):
                        pe.wait_ge(s["xn_ready"], NT * (it + 3))
                        wait(pe, s["v_copied"], it + 2)
                        wait(pe, s["osp_ready"], NT * it)
                        wait(pe, s["xT_copied"], it + 3)
                        for t in range(NT):
                            last = nc.tensor.transpose(work_ps[:, t * P:(t + 1) * P], xn[:, t, :], ident[:])
                        last.then_inc(s["w_xT"], 1)
                    if u_ == 7:
                        if exists(it - 1):
                            pe.wait_ge(s["osum_ready"], it)
                            wait(pe, s["xT_copied"], it + 4 if exists(it + 2) else 0)
                            for t in range(NT):
                                last = nc.tensor.transpose(work_ps[:, t * P:(t + 1) * P], o_sum[:, t, :], ident[:])
                            last.then_inc(s["w_osT"], 1)
                        if exists(it + 2):
                            pe.wait_ge(s["xT_copied"], it + 4)
                            wait(pe, s["osT_copied"], it)
                            if isinstance(it, int) and it == -2:
                                pe.wait_ge(s["setup_v"], 1)
                            for t in range(NT):
                                dst = work_ps[:, t * 2 * C:(t + 1) * 2 * C]
                                mm(dst, xnT[:, par, t * P:(t + 1) * P], w_qk[:], start=True, stop=False)
                                last = mm(dst, ones_row[:], b_row[:, 0:2 * C], start=False, stop=True)
                            last.then_inc(s["w_qk_ready"], 1)
                        if exists(it - 1):
                            pe.wait_ge(s["osT_copied"], it)
                            wait(pe, s["raw_ready"], it + 3 if exists(it + 2) else 0)
                            for t in range(NT):
                                last = mm(work_ps[:, t * C:(t + 1) * C], osT[:, t * P:(t + 1) * P], w_proj[:],
                                          start=True, stop=True)
                            last.then_inc(s["w_proj_ready"], 1)

                for u_ in range(UNITS):
                    if exists(it if u_ < UNITS - 1 else it + 1):
                        scores(u_)
                    if u_ % 2 == 1 and exists(it if u_ >= 5 else it - 1):
                        product(u_)
                    if exists(it if u_ >= 3 else it - 1):
                        turn(u_)
                    jobs(u_)

            iterations(pe, body)


_NAMES = ["L0_attn_x", "L0_attn_Wqkv", "L0_attn_bqkv", "L0_attn_q_gamma", "L0_attn_q_beta", "L0_attn_k_gamma",
          "L0_attn_k_beta", "L0_attn_alpha", "L0_attn_Wproj", "L0_attn_bproj", "L0_ffn_W", "L0_ffn_b",
          "L0_ffn_logits", "L0_ffn_u"]


def kernel(**inputs):
    import concourse.bacc as bacc
    from concourse.bass_utils import run_bass_kernel_spmd

    nc = bacc.Bacc("TRN2", target_bir_lowering=False, num_devices=1)
    arrays, args = {}, []
    for name in _NAMES:
        a = np.ascontiguousarray(inputs[name])
        arrays[f"in_{name}"] = a
        args.append(nc.dram_tensor(f"in_{name}", a.shape, mybir.dt.from_np(a.dtype), kind="ExternalInput").ap())
    shape = arrays["in_L0_attn_x"].shape
    args.append(nc.dram_tensor("out_y", shape, F32, kind="ExternalOutput").ap())
    build(nc, *args)
    result = run_bass_kernel_spmd(nc, [arrays], core_ids=[0])
    return result.results[0]["out_y"]
```

```python
from contextlib import ExitStack

import numpy as np

import concourse.bass as bass
from concourse import mybir

F32 = mybir.dt.float32
BF16 = mybir.dt.bfloat16
ALU = mybir.AluOpType
ACT = mybir.ActivationFunctionType
AX_X = mybir.AxisListType.X

P = 128
H = 16
D = 8
C = H * D
N = 256
NT = N // P
TOPK = max(1, int(N * 0.05))
LN_EPS = 1e-5
SUM_EPS = 1e-8
Z_EPS = 1e-6
SCORE_SCALE = float(1.0 / np.sqrt(np.float32(D)))
UNITS = H // 2
TILES = 4
QUADS = H // 4
VW = 32
VA = D + 1
REMOVED = -1.0
HUGE = float(2 ** 40)
PARTS = 3
SLOTS = [(0, 0), (0, 1), (0, 2), (1, 0), (1, 1), (1, 2), (2, 0), (2, 1)]
ROWS = len(SLOTS) * D
POOL_TILES = 3


def wait(engine, semaphore, value):
    if isinstance(value, int) and value <= 0:
        return None
    return engine.wait_ge(semaphore, value)


def wait_alone(engine, semaphore, value, passed):
    w = wait(engine, semaphore, value)
    if w is not None:
        w.then_inc(passed, 1)


def build(nc, x, Wqkv, bqkv, q_gamma, q_beta, k_gamma, k_beta, alpha, Wproj, bproj, W, bW, logits, u, y):
    B = x.shape[0]
    OPS = W.shape[0]
    assert x.shape[1:] == (N, C) and 2 * ROWS == P

    scratch = nc.dram_tensor("part_slots", (2, H * ROWS, N), BF16, kind="Internal").ap()
    x_t = x.rearrange("b (t p) c -> b p t c", p=P)
    y_t = y.rearrange("b (t p) c -> b p t c", p=P)

    def exists(batch):
        return not isinstance(batch, int) or 0 <= batch < B

    with ExitStack() as ctx:
        def sb(name, shape, dt=F32):
            return ctx.enter_context(nc.sbuf_tensor(name, shape, dt))

        def ps(name, shape, dt=F32):
            return ctx.enter_context(nc.psum_tensor(name, shape, dt))

        def sem(name):
            return ctx.enter_context(nc.semaphore(name))

        ident = sb("ident", [P, P])
        minus_huge = sb("minus_huge", [P, P], BF16)
        own_head = sb("own_head", [P, H, VA])
        ones_row = sb("ones_row", [1, P])
        w_in = sb("w_in", [P, 4, P])
        w_qk = sb("w_qk", [P, 2 * C])
        w_v = sb("w_v", [P, C])
        w_proj = sb("w_proj", [P, C])
        w_mean = sb("w_mean", [P, 2 * H])
        b_row = sb("b_row", [1, 3 * C])
        b_mean = sb("b_mean", [1, 2 * H])
        b_out = sb("b_out", [1, C])
        w_ops = sb("w_ops", [P, OPS, C])
        b_ops = sb("b_ops", [1, OPS, C])
        w_sel = sb("w_sel", [P, C])
        b_sel = sb("b_sel", [1, C])
        gate = sb("gate", [P, 12, OPS])
        gamma_in = sb("gamma_in", [P, 2, D])
        beta_in = sb("beta_in", [P, 2, D])
        gamma = sb("gamma", [P, 2, H, D])
        beta = sb("beta", [P, 2, H, D])
        mix = sb("mix", [P, 4, H])

        x_sb = sb("x_sb", [P, 2, NT, C])
        stats = sb("stats", [P, NT, 6])
        x_mv = sb("x_mv", [P, NT, 2])
        x_ln = sb("x_ln", [P, NT])
        x_rstd = sb("x_rstd", [P, NT])
        xn = sb("xn", [P, NT, C])
        xnT = sb("xnT", [P, 2, N])
        qk_sq = sb("qk_sq", [P, NT * 2 * C])
        qk_raw = sb("qk_raw", [P, NT * 2 * C])
        qk_ss = sb("qk_ss", [P, NT * 2 * H])
        qk_ln = sb("qk_ln", [P, NT * 2 * H])
        qk_rstd = sb("qk_rstd", [P, NT * 2 * H])
        qk_a = sb("qk_a", [P, NT * 2 * C])
        qk_b = sb("qk_b", [P, NT * 2 * C])
        qkn = sb("qkn", [P, NT * 2 * C])
        qkT = sb("qkT", [P, 2, N])
        residue = sb("residue", [P, 2, 2, N])
        part = sb("part", [P, PARTS, 2, N], BF16)
        q_slots = sb("q_slots", [P, 2, UNITS, N], BF16)
        k_slots = sb("k_slots", [P, 2, UNITS, N], BF16)
        d_max = sb("d_max", [P, NT * 2 * H])
        d_sub = sb("d_sub", [P, NT * 2 * C])
        d_exp = sb("d_exp", [P, NT * 2 * C])
        d_sum = sb("d_sum", [P, NT * 2 * H])
        d_rec = sb("d_rec", [P, NT * 2 * H])
        feat = sb("feat", [P, NT, 2, C])
        v_aug = sb("v_aug", [P, 2, NT, H, VW])
        kv = sb("kv", [P, H, VA])
        qfT = sb("qfT", [P, N])
        lin_z = sb("lin_z", [P, 3, NT, H])
        lin = sb("lin", [P, 2, NT, C])
        ffn = sb("ffn", [P, NT, C])
        base = sb("base", [P, 2, NT, C])

        top8 = sb("top8", [P, 2, TILES, 8])
        drop8 = sb("drop8", [P, 2, TILES, 8])
        e8 = sb("e8", [P, 2, TILES, 8])
        next8 = sb("next8", [P, 4, TILES, 8])
        rest = sb("rest", [P, TILES, N])
        negmax = sb("negmax", [P, 2, TILES])
        e = sb("e", [P, 4, TILES, N])
        below = sb("below", [P, 4, TILES, N], BF16)
        kept = sb("kept", [P, 4, 2, NT, N])
        z = sb("z", [P, 2, NT, H])

        oT = sb("oT", [P, 2, QUADS, N])
        den = sb("den", [P, 3, NT, H])
        o_sparse = sb("o_sparse", [P, NT, C])
        o_sum = sb("o_sum", [P, NT, C])
        osT = sb("osT", [P, N])
        proj = sb("proj", [P, NT, C])
        out_sb = sb("out_sb", [P, NT, C])

        score_ps = ps("score_ps", [P, 2, 2, NT, N])
        turn_ps = ps("turn_ps", [P, 2, NT, N])
        pv_ps = ps("pv_ps", [P, 512])
        work_ps = ps("work_ps", [P, 512])

        names = """const_loaded w_loaded x_loaded y_stored pool_const pool_step setup_v setup_a setup_p gate_step
            scores_ready top_ready negmax_ready rest_ready next_ready drop_ready e8_ready waits_passed
            exp_done below_pool below_act turn_ready turn_copied pv_ready pv_copied
            x_stats x_mean x_logged x_rstd_ready xn_ready
            w_xT xT_copied w_qk_ready sq_ready raw_ready ss_ready qk_logged qk_rstd_ready
            n_step qkn_ready w_qkT qkT_copied part_ready residue_ready slots_written slots_loaded
            dmax_ready dsub_ready dexp_ready dsum_ready drec_ready feat_ready
            w_v_ready v_copied w_kv kv_ready w_qfT qfT_copied w_lin linz_step lin_ready
            w_ffn ffn_copied base_ready
            w_turn den_step osp_ready osum_ready w_osT osT_copied w_proj_ready proj_copied
            y_ready""".split()
        s = {n: sem(n) for n in names}

        block = ctx.enter_context(nc.Block())

        def iterations(engine, body):
            first, last = 2, B - 2
            for it in range(-2, first):
                body(it, it % 2)
            with engine.Fori(first, last - 1, 2) as i:
                body(i, 0)
                body(i + 1, 1)
            for it in range(last, B + 2):
                body(it, it % 2)
        assert B % 2 == 0 and B >= 6

        @block.sync
        def _(sp):
            for i, src in enumerate((Wqkv[0:P], Wqkv[P:2 * P], Wqkv[2 * P:3 * P], Wproj)):
                sp.dma_start(w_in[:, i, :], src).then_inc(s["w_loaded"], 16)
            for b in range(2):
                sp.dma_start(x_sb[:, b], x_t[b]).then_inc(s["x_loaded"], 16)
            sp.dma_start(b_row[:, :], bqkv.rearrange("(o c) -> o c", o=1)).then_inc(s["const_loaded"], 16)
            sp.dma_start(b_out[:, :], bproj.rearrange("(o c) -> o c", o=1)).then_inc(s["const_loaded"], 16)
            for i, (g_in, b_in) in enumerate(((q_gamma, q_beta), (k_gamma, k_beta))):
                sp.dma_start(gamma_in[:, i, :], g_in.partition_broadcast(P)).then_inc(s["const_loaded"], 16)
                sp.dma_start(beta_in[:, i, :], b_in.partition_broadcast(P)).then_inc(s["const_loaded"], 16)
            sp.dma_start(mix[:, 0, :], alpha.partition_broadcast(P)).then_inc(s["const_loaded"], 16)
            sp.dma_start(gate[:, 0, :], logits.partition_broadcast(P)).then_inc(s["const_loaded"], 16)
            sp.dma_start(gate[:, 1, :], u.partition_broadcast(P)).then_inc(s["const_loaded"], 16)
            sp.dma_start(w_ops[:, :, :], W.rearrange("o d e -> d o e")).then_inc(s["const_loaded"], 16)
            sp.dma_start(b_ops[:, :, :], bW.rearrange("(a o) e -> a o e", a=1)).then_inc(s["const_loaded"], 16)

            def body(it, par):
                nxt = 1 - par
                if exists(it - 2):
                    wait_alone(sp, s["y_ready"], it - 1, s["waits_passed"])
                    sp.dma_start(y_t[it - 2], out_sb[:]).then_inc(s["y_stored"], 16)
                if exists(it + 2) and not (isinstance(it, int) and it < 0):
                    wait_alone(sp, s["base_ready"], it + 1, s["waits_passed"])
                    sp.dma_start(x_sb[:, par], x_t[it + 2]).then_inc(s["x_loaded"], 16)
                if exists(it + 1):
                    wait_alone(sp, s["slots_loaded"], 32 * (it + 1), s["waits_passed"])
                    for p in range(PARTS):
                        wait_alone(sp, s["part_ready"], PARTS * (it + 1) + p + 1, s["waits_passed"])
                        for slot, parts in enumerate(SLOTS):
                            for side in range(2):
                                if parts[side] == p:
                                    dst = scratch[side].rearrange("(h s d) n -> s h d n", h=H, d=D)[slot]
                                    sp.dma_start(dst, part[:, p, side, :]).then_inc(s["slots_written"], 16)
                    wait_alone(sp, s["slots_written"], 16 * 2 * len(SLOTS) * (it + 2), s["waits_passed"])
                    wait_alone(sp, s["scores_ready"], UNITS * it, s["waits_passed"])
                    for side, dst in enumerate((q_slots, k_slots)):
                        sp.dma_start(dst[:, nxt], scratch[side].rearrange("(g p) n -> p g n", p=P)).then_inc(
                            s["slots_loaded"], 16)

            iterations(sp, body)
            sp.wait_ge(s["y_stored"], 16 * B)

        @block.gpsimd
        def _(pool):
            def select(out, op, fill, base_, pattern, mult, n):
                pool.wait_ge(s["pool_step"], n)
                return nc.gpsimd.affine_select(out=out, in_=out, compare_op=op, fill=fill, base=base_,
                                               pattern=pattern, channel_multiplier=mult)
            nc.gpsimd.memset(ident[:], 0.0).then_inc(s["pool_step"], 1)
            nc.gpsimd.memset(minus_huge[:], 0.0).then_inc(s["pool_step"], 1)
            nc.gpsimd.memset(own_head[:], 1.0).then_inc(s["pool_step"], 1)
            nc.gpsimd.memset(ones_row[:], 1.0).then_inc(s["pool_const"], 1)
            nc.gpsimd.memset(v_aug[:], 0.0).then_inc(s["pool_step"], 1)
            select(ident[:], ALU.not_equal, 1.0, 0, [[-1, P]], 1, 4).then_inc(s["pool_const"], 1)
            select(minus_huge[:], ALU.not_equal, -HUGE, 0, [[-1, P]], 1, 4).then_inc(s["pool_const"], 1)
            select(own_head[:], ALU.is_ge, 0.0, 0, [[-D, H], [0, VA]], 1, 4).then_inc(s["pool_step"], 1)
            select(own_head[:], ALU.is_ge, 0.0, D - 1, [[D, H], [0, VA]], -1, 5).then_inc(s["pool_const"], 1)
            for par in range(2):
                nc.gpsimd.memset(v_aug[:, par, :, :, D:VA], 1.0).then_inc(s["pool_const"], 1)
            pool.wait_ge(s["setup_v"], 5)
            gb = gamma[:].rearrange("p a h d -> p (a h d)")
            bb = beta[:].rearrange("p a h d -> p (a h d)")

            def halves(ap):
                return ap.rearrange("p (t f) -> p t f", t=NT)

            def heads(ap):
                return ap.rearrange("p (g d) -> p g d", d=D)

            def spread(ap):
                return ap.unsqueeze(2).to_broadcast([P, NT * 2 * H, D])

            def normalise(it, n):
                if n == 0:
                    pool.wait_ge(s["raw_ready"], it + 2)
                    pool.wait_ge(s["qk_rstd_ready"], it + 2)
                    nc.gpsimd.tensor_tensor(heads(qk_a[:]), heads(qk_raw[:]), spread(qk_rstd[:]),
                                            ALU.mult).then_inc(s["n_step"], 1)
                else:
                    pool.wait_ge(s["n_step"], 2 * (it + 1) + n)
                    dst, src, other, op, done = (
                        (qk_b, qk_a, gb, ALU.mult, "n_step"), (qkn, qk_b, bb, ALU.add, "qkn_ready"))[n - 1]
                    nc.gpsimd.tensor_tensor(halves(dst[:]), halves(src[:]),
                                            other.unsqueeze(1).to_broadcast([P, NT, 2 * C]),
                                            op).then_inc(s[done], 1)

            def leave(it, p):
                pool.wait_ge(s["part_ready"], PARTS * (it + 1) + p + 1)
                if p == 0:
                    pool.wait_ge(s["qkT_copied"], it + 2)
                else:
                    pool.wait_ge(s["residue_ready"], 2 * (it + 1) + 1)
                src = qkT[:] if p == 0 else residue[:, 0]
                nc.gpsimd.tensor_tensor(residue[:, p], src, part[:, p], ALU.subtract).then_inc(s["residue_ready"], 1)

            def body(it, par):
                nxt = 1 - par
                for u_ in range(UNITS):
                    g = it * UNITS + u_
                    if u_ == 1 and exists(it + 1):
                        normalise(it, 0)
                    if u_ == 5 and exists(it + 1):
                        leave(it, 1)
                    if exists(it if u_ >= 2 else it - 1):
                        r = (u_ - 2) % 4
                        for t in range(POOL_TILES):
                            wait_alone(pool, s["next_ready"], TILES * (g - 2) + t + 1, s["waits_passed"])
                            nc.gpsimd.tensor_scalar(below[:, r, t, :], e[:, r, t, :],
                                                    next8[:, r, t, TOPK - 9:TOPK - 8], None,
                                                    ALU.is_lt).then_inc(s["below_pool"], 1)
                    if u_ == 1 and exists(it + 1):
                        normalise(it, 1)
                    if u_ == 1 and exists(it - 2):
                        pool.wait_ge(s["proj_copied"], it - 1)
                        wait(pool, s["y_stored"], 16 * (it - 2))
                        nc.gpsimd.tensor_tensor(out_sb[:], proj[:], base[:, par], ALU.add).then_inc(s["y_ready"], 1)
                    if u_ == 2 and exists(it + 1):
                        normalise(it, 2)
                    if u_ == 2 and exists(it):
                        pool.wait_ge(s["ffn_copied"], it + 1)
                        wait(pool, s["y_ready"], it - 1)
                        nc.gpsimd.tensor_tensor(base[:, par], ffn[:], x_sb[:, par],
                                                ALU.add).then_inc(s["base_ready"], 1)
                    if u_ == 3 and exists(it + 1):
                        pool.wait_ge(s["dmax_ready"], it + 2)
                        nc.gpsimd.tensor_tensor(heads(d_sub[:]), heads(qkn[:]), spread(d_max[:]),
                                                ALU.subtract).then_inc(s["dsub_ready"], 1)
                        leave(it, 0)
                    if u_ == 7 and exists(it - 1):
                        pool.wait_ge(s["osp_ready"], NT * it)
                        pool.wait_ge(s["lin_ready"], it)
                        nc.gpsimd.tensor_tensor(o_sum[:], o_sparse[:], lin[:, nxt],
                                                ALU.add).then_inc(s["osum_ready"], 1)
                    if u_ == 7 and exists(it + 1):
                        pool.wait_ge(s["drec_ready"], it + 2)
                        pool.wait_ge(s["dexp_ready"], 2 * (it + 2))
                        nc.gpsimd.tensor_tensor(heads(feat[:].rearrange("p t a c -> p (t a c)")), heads(d_exp[:]),
                                                spread(d_rec[:]), ALU.mult).then_inc(s["feat_ready"], 1)

            iterations(pool, body)

        @block.vector
        def _(dve):
            step = [0]

            def setup(ins):
                step[0] += 1
                ins.then_inc(s["setup_p"], 1)
                dve.wait_ge(s["setup_p"], step[0])

            dve.wait_ge(s["setup_a"], 1)
            wq4 = w_qk[:].rearrange("p (g d) -> p g d", d=D)
            setup(nc.vector.tensor_reduce(w_mean[:], wq4, AX_X, ALU.add))
            setup(nc.vector.tensor_scalar(w_mean[:], w_mean[:], 1.0 / D, None, ALU.mult))
            setup(nc.vector.tensor_tensor(wq4, wq4, w_mean[:].unsqueeze(2).to_broadcast([P, 2 * H, D]), ALU.subtract))
            dve.wait_ge(s["const_loaded"], 16 * 11)
            bq4 = b_row[:, 0:2 * C].rearrange("p (g d) -> p g d", d=D)
            setup(nc.vector.tensor_reduce(b_mean[:], bq4, AX_X, ALU.add))
            setup(nc.vector.tensor_scalar(b_mean[:], b_mean[:], 1.0 / D, None, ALU.mult))
            nc.vector.tensor_tensor(bq4, bq4, b_mean[:].unsqueeze(2).to_broadcast([1, 2 * H, D]),
                                    ALU.subtract).then_inc(s["setup_v"], 1)
            dve.wait_ge(s["setup_v"], 1)
            for i, factor in enumerate((SCORE_SCALE, 1.0)):
                for dst, src in ((gamma, gamma_in), (beta, beta_in)):
                    nc.vector.tensor_scalar(dst[:, i], src[:, i].unsqueeze(1).to_broadcast([P, H, D]), factor, None,
                                            ALU.mult).then_inc(s["setup_v"], 1)

            def stage_gate():
                setup(nc.vector.reduce_max(gate[:, 2, 0:1], gate[:, 0, :], AX_X))
                nc.vector.tensor_scalar(gate[:, 3, :], gate[:, 0, :], gate[:, 2, 0:1], None,
                                        ALU.subtract).then_inc(s["setup_v"], 1)
                for i in range(OPS):
                    last = nc.vector.memset(gate[:, 4, i:i + 1], float(OPS - i))
                setup(last)
                dve.wait_ge(s["setup_a"], 2)
                dve.wait_ge(s["setup_v"], 6)
                setup(nc.vector.tensor_scalar(gate[:, 3, :], gate[:, 3, :], gate[:, 5, 1:2], None, ALU.subtract))
                setup(nc.vector.tensor_tensor(gate[:, 3, :], gate[:, 3, :], gate[:, 6, :], ALU.subtract))
                setup(nc.vector.reduce_max(gate[:, 2, 1:2], gate[:, 3, :], AX_X))
                setup(nc.vector.scalar_tensor_tensor(out=gate[:, 7, :], in0=gate[:, 3, :], scalar=gate[:, 2, 1:2],
                                                     in1=gate[:, 4, :], op0=ALU.is_ge, op1=ALU.mult))
                setup(nc.vector.reduce_max(gate[:, 2, 2:3], gate[:, 7, :], AX_X))
                setup(nc.vector.tensor_scalar(gate[:, 8, :], gate[:, 7, :], gate[:, 2, 2:3], None, ALU.is_ge))
                for dst, src, one in ((w_sel, w_ops, gate), (b_sel, b_ops, gate[0:1])):
                    setup(nc.vector.tensor_scalar(dst[:], src[:, 0, :], one[:, 8, 0:1], None, ALU.mult))
                    for i in range(1, OPS):
                        setup(nc.vector.scalar_tensor_tensor(out=dst[:], in0=src[:, i, :], scalar=one[:, 8, i:i + 1],
                                                             in1=dst[:], op0=ALU.mult, op1=ALU.add))
                nc.vector.tensor_tensor(b_out[:], b_out[:], b_sel[:], ALU.add).then_inc(s["setup_v"], 1)
                setup(nc.vector.tensor_scalar(mix[:, 1, :], mix[:, 1, :], 1.0, None, ALU.add))
                setup(nc.vector.reciprocal(mix[:, 2, :], mix[:, 1, :]))
                setup(nc.vector.tensor_scalar(mix[:, 3, :], mix[:, 2, :], -1.0, 1.0, ALU.mult, ALU.add))

            def alone(semaphore, value):
                wait_alone(dve, semaphore, value, s["waits_passed"])

            def body(it, par):
                nxt = 1 - par

                def top(g, q, t):
                    alone(s["scores_ready"], g + 1)
                    nc.vector.max(top8[:, q, t, :], score_ps[:, q, t // 2, t % 2, :]).then_inc(s["top_ready"], 1)

                def remove(u_, t):
                    g1 = it * UNITS + u_ - 1
                    wait(dve, s["next_ready"], TILES * (g1 - 1) + t + 1)
                    alone(s["e8_ready"], g1 + 1)
                    nc.vector.match_replace(rest[:, t, :], e8[:, (u_ - 1) % 2, t, :], e[:, (u_ - 1) % 4, t, :],
                                            REMOVED).then_inc(s["rest_ready"], 1)

                def following(u_, t):
                    alone(s["rest_ready"], TILES * (it * UNITS + u_ - 1) + t + 1)
                    nc.vector.max(next8[:, (u_ - 1) % 4, t, :], rest[:, t, :]).then_inc(s["next_ready"], 1)

                def extra(u_, k):
                    if u_ == 0 and k == 0 and exists(it + 1):
                        dve.wait_ge(s["sq_ready"], it + 2)
                        nc.vector.tensor_reduce(qk_ss[:], qk_sq[:].rearrange("p (g d) -> p g d", d=D), AX_X,
                                                ALU.add).then_inc(s["ss_ready"], 1)
                    if u_ == 2 and k == 1 and exists(it):
                        dve.wait_ge(s["w_kv"], it + 1)
                        if isinstance(it, int) and it == 0:
                            dve.wait_ge(s["pool_const"], 6)
                        nc.vector.tensor_tensor(kv[:], work_ps[:, 0:H * VA].rearrange("p (h e) -> p h e", e=VA),
                                                own_head[:], ALU.mult).then_inc(s["kv_ready"], 1)
                    if u_ == 5 and 1 <= k <= 4 and exists(it):
                        w = work_ps[:, 0:NT * H * VA].rearrange("p (t h e) -> p t h e", t=NT, e=VA)
                        if k == 1:
                            dve.wait_ge(s["w_lin"], it + 1)
                            nc.vector.tensor_scalar(lin_z[:, 0], w[:, :, :, D], Z_EPS, None,
                                                    ALU.add).then_inc(s["linz_step"], 1)
                        if k == 2:
                            dve.wait_ge(s["linz_step"], 3 * it + 1)
                            nc.vector.reciprocal(lin_z[:, 1], lin_z[:, 0]).then_inc(s["linz_step"], 1)
                        if k == 3:
                            dve.wait_ge(s["linz_step"], 3 * it + 2)
                            nc.vector.tensor_tensor(lin_z[:, 2], lin_z[:, 1],
                                                    mix[:, 3, :].unsqueeze(1).to_broadcast([P, NT, H]),
                                                    ALU.mult).then_inc(s["linz_step"], 1)
                        if k == 4:
                            dve.wait_ge(s["linz_step"], 3 * it + 3)
                            nc.vector.tensor_tensor(
                                lin[:, par].rearrange("p t (h d) -> p (t h) d", d=D),
                                work_ps[:, 0:NT * H * VA].rearrange("p (g e) -> p g e", e=VA)[:, :, 0:D],
                                lin_z[:, 2].rearrange("p t h -> p (t h)").unsqueeze(2).to_broadcast([P, NT * H, D]),
                                ALU.mult).then_inc(s["lin_ready"], 1)
                    if u_ == 3 and k == 0 and exists(it + 1):
                        dve.wait_ge(s["qkn_ready"], it + 2)
                        nc.vector.tensor_reduce(d_max[:], qkn[:].rearrange("p (g d) -> p g d", d=D), AX_X,
                                                ALU.max).then_inc(s["dmax_ready"], 1)
                    if u_ in (4, 6) and 1 <= k <= 4 and exists(it - 1):
                        t = (u_ - 4) // 2
                        w = pv_ps[:].rearrange("p (h e) -> p h e", e=VW)
                        n = 3 * (NT * (it - 1) + t)
                        if k == 1:
                            dve.wait_ge(s["w_turn"], NT * (it - 1) + t + 1)
                            nc.vector.scalar_tensor_tensor(out=den[:, 0, t], in0=z[:, nxt, t], scalar=SUM_EPS,
                                                           in1=w[:, :, D], op0=ALU.mult,
                                                           op1=ALU.add).then_inc(s["den_step"], 1)
                        if k == 2:
                            dve.wait_ge(s["den_step"], n + 1)
                            nc.vector.reciprocal(den[:, 1, t], den[:, 0, t]).then_inc(s["den_step"], 1)
                        if k == 3:
                            dve.wait_ge(s["den_step"], n + 2)
                            nc.vector.tensor_tensor(den[:, 2, t], den[:, 1, t], mix[:, 2, :],
                                                    ALU.mult).then_inc(s["den_step"], 1)
                        if k == 4:
                            dve.wait_ge(s["den_step"], n + 3)
                            nc.vector.tensor_tensor(o_sparse[:, t].rearrange("p (h d) -> p h d", d=D), w[:, :, 0:D],
                                                    den[:, 2, t].unsqueeze(2).to_broadcast([P, H, D]),
                                                    ALU.mult).then_inc(s["osp_ready"], 1)
                    if u_ == 4 and exists(it + 2):
                        if k == 0:
                            dve.wait_ge(s["x_loaded"], 16 * (it + 3))
                            for t in range(NT):
                                nc.vector.bn_stats(stats[:, t], x_sb[:, par, t]).then_inc(s["x_stats"], 1)
                        if k == 5:
                            alone(s["x_stats"], NT * (it + 3))
                            for t in range(NT):
                                nc.vector.bn_aggr(x_mv[:, t], stats[:, t]).then_inc(s["x_mean"], 1)
                    if u_ == 5 and exists(it + 1):
                        if k == 5:
                            dve.wait_ge(s["dexp_ready"], 2 * (it + 2))
                            nc.vector.tensor_reduce(d_sum[:], d_exp[:].rearrange("p (g d) -> p g d", d=D), AX_X,
                                                    ALU.add).then_inc(s["dsum_ready"], 1)
                    if u_ == 6 and exists(it + 1) and k == 5:
                        dve.wait_ge(s["dsum_ready"], it + 2)
                        nc.vector.reciprocal(d_rec[:], d_sum[:]).then_inc(s["drec_ready"], 1)
                    if u_ == 6 and exists(it + 2) and k == 0:
                        dve.wait_ge(s["x_rstd_ready"], it + 3)
                        wait(dve, s["w_xT"], it + 3)
                        for t in range(NT):
                            nc.vector.tensor_scalar(xn[:, t], x_sb[:, par, t], x_mv[:, t, 0:1], x_rstd[:, t:t + 1],
                                                    ALU.subtract, ALU.mult).then_inc(s["xn_ready"], 1)

                if isinstance(it, int) and it == -1:
                    stage_gate()
                for u_ in range(UNITS):
                    g = it * UNITS + u_
                    q = u_ % 2
                    before = exists(it if u_ else it - 1)
                    if exists(it):
                        for t in range(TILES):
                            top(g, q, t)
                    if before:
                        remove(u_, 0)
                    if exists(it):
                        dve.wait_ge(s["top_ready"], TILES * (g + 1))
                        nc.vector.tensor_scalar(negmax[:, q, :], top8[:, q, :, 0], -1.0, None,
                                                ALU.mult).then_inc(s["negmax_ready"], 1)
                        nc.vector.tensor_tensor(drop8[:, q], top8[:, q], top8[:, q, :, 0:1].to_broadcast(
                            [P, TILES, 8]), ALU.subtract).then_inc(s["drop_ready"], 1)
                    extra(u_, 0)
                    if before:
                        remove(u_, 1)
                    extra(u_, 1)
                    if before:
                        following(u_, 0)
                    extra(u_, 2)
                    if before:
                        remove(u_, 2)
                    extra(u_, 3)
                    if before:
                        following(u_, 1)
                    extra(u_, 4)
                    if before:
                        remove(u_, 3)
                        following(u_, 2)
                    extra(u_, 5)
                    if before:
                        following(u_, 3)

            iterations(dve, body)

        @block.scalar
        def _(act):
            nc.scalar.preload_act_table_set("natural_log_exp_and_others")
            act.wait_ge(s["w_xT"], 1)
            nc.scalar.copy(w_qk[:], work_ps[:, 0:2 * C]).then_inc(s["setup_a"], 1)
            nc.scalar.copy(w_v[:], work_ps[:, 2 * C:3 * C])
            nc.scalar.copy(w_proj[:], work_ps[:, 3 * C:4 * C]).then_inc(s["xT_copied"], 1)

            def stage_gate():
                act.wait_ge(s["setup_v"], 6)
                nc.scalar.activation(gate[:, 9, :], gate[:, 3, :], ACT.Exp,
                                     accum_out=gate[:, 5, 0:1]).then_inc(s["gate_step"], 1)
                nc.scalar.activation(gate[:, 10, :], gate[:, 1, :], ACT.Ln).then_inc(s["gate_step"], 1)
                nc.scalar.activation(mix[:, 1, :], mix[:, 0, :], ACT.Exp, scale=-1.0).then_inc(s["gate_step"], 1)
                act.wait_ge(s["gate_step"], 3)
                nc.scalar.activation(gate[:, 5, 1:2], gate[:, 5, 0:1], ACT.Ln)
                nc.scalar.activation(gate[:, 6, :], gate[:, 10, :], ACT.Ln, scale=-1.0).then_inc(s["setup_a"], 1)

            def body(it, par):
                nxt = 1 - par
                if isinstance(it, int) and it == -1:
                    stage_gate()
                for u_ in range(UNITS):
                    g = it * UNITS + u_
                    if exists(it if u_ >= 2 else it - 1):
                        r = (u_ - 2) % 4
                        act.wait_ge(s["next_ready"], TILES * (g - 1))
                        for t in range(POOL_TILES, TILES):
                            nc.scalar.activation(below[:, r, t, :], e[:, r, t, :], ACT.Relu, scale=-1.0,
                                                 bias=next8[:, r, t, TOPK - 9:TOPK - 8]).then_inc(s["below_act"], 1)

                    if exists(it if u_ >= 3 else it - 1):
                        wait(act, s["pv_ready"], it * QUADS + (u_ - 7) // 2 + 1)
                        for hh in range(2):
                            act.wait_ge(s["turn_ready"], 2 * (g - 3) + hh + 1)
                            nc.scalar.activation(kept[:, (u_ - 3) % 4, hh], turn_ps[:, hh], ACT.Relu).then_inc(
                                s["turn_copied"], 1)

                    if u_ == 0 and exists(it - 2):
                        act.wait_ge(s["w_osT"], it - 1)
                        nc.scalar.copy(osT[:], work_ps[:, 0:N]).then_inc(s["osT_copied"], 1)
                    if u_ == 1 and exists(it - 2):
                        act.wait_ge(s["w_proj_ready"], it - 1)
                        wait(act, s["y_ready"], it - 2)
                        nc.scalar.copy(proj[:], work_ps[:, 0:NT * C].rearrange("p (t c) -> p t c", t=NT)).then_inc(
                            s["proj_copied"], 1)
                    if u_ == 3 and exists(it + 1):
                        act.wait_ge(s["w_qkT"], it + 2)
                        wait(act, s["residue_ready"], 2 * (it + 1))
                        nc.scalar.copy(qkT[:], work_ps[:].rearrange("p (a n) -> p a n", a=2)).then_inc(
                            s["qkT_copied"], 1)
                        wait(act, s["slots_written"], 16 * 2 * len(SLOTS) * (it + 1))
                        nc.scalar.copy(part[:, 0], work_ps[:].rearrange("p (a n) -> p a n", a=2)).then_inc(
                            s["part_ready"], 1)
                    if u_ == 6 and exists(it + 1):
                        act.wait_ge(s["w_v_ready"], it + 2)
                        nc.scalar.copy(v_aug[:, nxt, :, :, 0:D].rearrange("p t h d -> p (t h) d"),
                                       work_ps[:, 0:NT * C].rearrange("p (g d) -> p g d", d=D)).then_inc(
                                           s["v_copied"], 1)

                    if exists(it):
                        act.wait_ge(s["negmax_ready"], g + 1)
                        if u_ == 0:
                            wait(act, s["osp_ready"], NT * (it - 1))
                        wait(act, s["turn_ready"], 2 * (g - 3))
                        for t in range(TILES):
                            nc.scalar.activation(e[:, u_ % 4, t, :], score_ps[:, u_ % 2, t // 2, t % 2, :], ACT.Exp,
                                                 bias=negmax[:, u_ % 2, t:t + 1],
                                                 accum_out=z[:, par, t % 2, 2 * u_ + t // 2:2 * u_ + t // 2 + 1]
                                                 ).then_inc(s["exp_done"], 1)
                        act.wait_ge(s["drop_ready"], g + 1)
                        nc.scalar.activation(e8[:, u_ % 2], drop8[:, u_ % 2], ACT.Exp).then_inc(s["e8_ready"], 1)

                    if u_ % 2 == 1 and exists(it if u_ >= 5 else it - 1):
                        act.wait_ge(s["pv_ready"], it * QUADS + (u_ - 5) // 2 + 1)
                        if u_ == 5:
                            wait(act, s["w_turn"], NT * (it - 1))
                        nc.scalar.copy(oT[:, par if u_ >= 5 else nxt, (u_ - 5) // 2 % 4], pv_ps[:, 0:N]).then_inc(
                            s["pv_copied"], 1)

                    if u_ == 0 and exists(it):
                        act.wait_ge(s["w_ffn"], it + 1)
                        wait(act, s["base_ready"], it)
                        nc.scalar.copy(ffn[:], work_ps[:, 0:NT * C].rearrange("p (t c) -> p t c", t=NT)).then_inc(
                            s["ffn_copied"], 1)
                    if u_ == 0 and exists(it + 1):
                        act.wait_ge(s["ss_ready"], it + 2)
                        nc.scalar.activation(qk_ln[:], qk_ss[:], ACT.Ln, scale=1.0 / D,
                                             bias=LN_EPS).then_inc(s["qk_logged"], 1)
                        act.wait_ge(s["qk_logged"], it + 2)
                        nc.scalar.activation(qk_rstd[:], qk_ln[:], ACT.Exp, scale=-0.5).then_inc(
                            s["qk_rstd_ready"], 1)
                    if u_ == 4 and exists(it):
                        act.wait_ge(s["w_qfT"], it + 1)
                        nc.scalar.copy(qfT[:], work_ps[:, 0:N]).then_inc(s["qfT_copied"], 1)
                    if u_ in (4, 5) and exists(it + 1):
                        p = u_ - 3
                        act.wait_ge(s["residue_ready"], 2 * (it + 1) + p)
                        nc.scalar.copy(part[:, p], residue[:, p - 1]).then_inc(s["part_ready"], 1)
                    if u_ == 4 and exists(it + 1):
                        act.wait_ge(s["dsub_ready"], it + 2)
                        sub = d_sub[:].rearrange("p (t a c) -> p t a c", t=NT, a=2)
                        dst = d_exp[:].rearrange("p (t a c) -> p t a c", t=NT, a=2)
                        for side, factor in enumerate((1.0 / SCORE_SCALE, 1.0)):
                            nc.scalar.activation(dst[:, :, side, :], sub[:, :, side, :], ACT.Exp,
                                                 scale=factor).then_inc(s["dexp_ready"], 1)
                    if u_ == 5 and exists(it + 2):
                        act.wait_ge(s["x_mean"], NT * (it + 3))
                        nc.scalar.activation(x_ln[:], x_mv[:, :, 1], ACT.Ln, bias=LN_EPS).then_inc(
                            s["x_logged"], 1)
                        act.wait_ge(s["x_logged"], it + 3)
                        nc.scalar.activation(x_rstd[:], x_ln[:], ACT.Exp, scale=-0.5).then_inc(
                            s["x_rstd_ready"], 1)
                    if u_ == 6 and exists(it + 2):
                        act.wait_ge(s["w_xT"], it + 4)
                        nc.scalar.copy(xnT[:, par], work_ps[:, 0:N]).then_inc(s["xT_copied"], 1)
                    if u_ == 7 and exists(it + 2):
                        act.wait_ge(s["w_qk_ready"], it + 3)
                        nc.scalar.activation(qk_sq[:], work_ps[:], ACT.Square).then_inc(s["sq_ready"], 1)
                        wait(act, s["n_step"], 2 * (it + 2))
                        nc.scalar.copy(qk_raw[:], work_ps[:]).then_inc(s["raw_ready"], 1)

            iterations(act, body)

        @block.tensor
        def _(pe):
            mm = nc.tensor.matmul
            pe.wait_ge(s["w_loaded"], 16 * 4)
            pe.wait_ge(s["pool_const"], 6)
            for i in range(4):
                last = nc.tensor.transpose(work_ps[:, i * P:(i + 1) * P], w_in[:, i, :], ident[:])
            last.then_inc(s["w_xT"], 1)

            def body(it, par):
                nxt = 1 - par

                def scores(u_):
                    g1 = it * UNITS + u_ + 1
                    side, v_ = (par, u_ + 1) if u_ < UNITS - 1 else (nxt, 0)
                    if v_ == 0:
                        pe.wait_ge(s["slots_loaded"], 32 * (it + 2))
                    wait_alone(pe, s["exp_done"], TILES * (g1 - 1), s["waits_passed"])
                    for t in range(TILES):
                        hh, nt = t // 2, t % 2
                        rows = slice(ROWS * hh, ROWS * (hh + 1))
                        last = mm(score_ps[:, v_ % 2, hh, nt, :], q_slots[rows, side, v_, nt * P:(nt + 1) * P],
                                  k_slots[rows, side, v_, :], start=True, stop=True)
                    last.then_inc(s["scores_ready"], 1)

                def turn(u_):
                    g2 = it * UNITS + u_ - 3
                    r = (u_ - 3) % 4
                    pe.wait_ge(s["below_pool"], POOL_TILES * (g2 + 1))
                    pe.wait_ge(s["below_act"], (TILES - POOL_TILES) * (g2 + 1))
                    for hh in range(2):
                        wait(pe, s["turn_copied"], 2 * (g2 - 1) + hh + 1)
                        for nt in range(NT):
                            t = 2 * hh + nt
                            for mc in range(NT):
                                dst = turn_ps[:, hh, mc, nt * P:(nt + 1) * P]
                                keys = slice(mc * P, (mc + 1) * P)
                                mm(dst, e[:, r, t, keys], ident[:], start=True, stop=False, is_transpose=True)
                                last = mm(dst, below[:, r, t, keys], minus_huge[:], start=False, stop=True)
                        last.then_inc(s["turn_ready"], 1)

                def product(u_):
                    quad = it * QUADS + (u_ - 5) // 2
                    side = par if u_ >= 5 else nxt
                    q = (u_ - 5) // 2 % 4
                    pe.wait_ge(s["turn_copied"], 4 * (quad + 1))
                    wait(pe, s["pv_copied"], quad)
                    if u_ >= 5:
                        wait(pe, s["osp_ready"], NT * (it - 1) + (u_ - 3) // 2)
                    for mc in range(NT):
                        for j in range(4):
                            v_ = 2 * q + j // 2
                            last = mm(pv_ps[32 * j:32 * (j + 1), 0:N], v_aug[:, side, mc, 4 * q + j, :],
                                      kept[:, v_ % 4, j % 2, mc, :], start=(mc == 0), stop=(mc == NT - 1),
                                      tile_position=(0, 32 * j))
                    last.then_inc(s["pv_ready"], 1)

                def sums(u_):
                    t = (u_ - 4) // 2
                    pe.wait_ge(s["pv_copied"], QUADS * it + (t if exists(it) else 0))
                    if t:
                        pe.wait_ge(s["osp_ready"], NT * (it - 1) + t)
                    for q in range(QUADS):
                        last = nc.tensor.transpose(pv_ps[:, q * P:(q + 1) * P],
                                                   oT[:, nxt, q, t * P:(t + 1) * P], ident[:])
                    last.then_inc(s["w_turn"], 1)

                def early(u_):
                    if u_ == 0 and exists(it - 2):
                        pe.wait_ge(s["osum_ready"], it - 1)
                        wait(pe, s["raw_ready"], it + 2 if exists(it + 1) else 0)
                        for t in range(NT):
                            last = nc.tensor.transpose(work_ps[:, t * P:(t + 1) * P], o_sum[:, t, :], ident[:])
                        last.then_inc(s["w_osT"], 1)
                    if u_ == 1 and exists(it - 2):
                        pe.wait_ge(s["osT_copied"], it - 1)
                        wait(pe, s["ffn_copied"], it + 1 if exists(it) else 0)
                        for t in range(NT):
                            last = mm(work_ps[:, t * C:(t + 1) * C], osT[:, t * P:(t + 1) * P], w_proj[:],
                                      start=True, stop=True)
                        last.then_inc(s["w_proj_ready"], 1)
                    if u_ == 3 and exists(it + 1):
                        wait(pe, s["kv_ready"], it + 1)
                        pe.wait_ge(s["qkn_ready"], it + 2)
                        for side in range(2):
                            for t in range(NT):
                                last = nc.tensor.transpose(
                                    work_ps[:, side * N + t * P:side * N + (t + 1) * P],
                                    qkn[:, (2 * t + side) * C:(2 * t + side + 1) * C], ident[:])
                        last.then_inc(s["w_qkT"], 1)
                    if u_ == 5 and exists(it):
                        pe.wait_ge(s["qfT_copied"], it + 1)
                        for t in range(NT):
                            last = mm(work_ps[:, t * H * VA:(t + 1) * H * VA], qfT[:, t * P:(t + 1) * P],
                                      kv[:].rearrange("p h e -> p (h e)"), start=True, stop=True)
                        last.then_inc(s["w_lin"], 1)
                    if u_ == 6 and exists(it + 1):
                        wait(pe, s["part_ready"], PARTS * (it + 1) + 1)
                        wait(pe, s["lin_ready"], it + 1)
                        for t in range(NT):
                            dst = work_ps[:, t * C:(t + 1) * C]
                            mm(dst, xnT[:, nxt, t * P:(t + 1) * P], w_v[:], start=True, stop=False)
                            last = mm(dst, ones_row[:], b_row[:, 2 * C:3 * C], start=False, stop=True)
                        last.then_inc(s["w_v_ready"], 1)

                def late(u_):
                    if u_ == 0 and exists(it):
                        pe.wait_ge(s["raw_ready"], it + 2 if exists(it + 1) else it + 1)
                        wait(pe, s["osT_copied"], it - 1)
                        pe.wait_ge(s["setup_v"], 7)
                        for t in range(NT):
                            dst = work_ps[:, t * C:(t + 1) * C]
                            mm(dst, xnT[:, par, t * P:(t + 1) * P], w_sel[:], start=True, stop=False)
                            last = mm(dst, ones_row[:], b_out[:], start=False, stop=True)
                        last.then_inc(s["w_ffn"], 1)
                    if u_ == 1 and exists(it):
                        pe.wait_ge(s["ffn_copied"], it + 1)
                        wait(pe, s["proj_copied"], it - 1)
                        pe.wait_ge(s["feat_ready"], it + 1)
                        for t in range(NT):
                            last = mm(work_ps[:, 0:H * VA], feat[:, t, 1, :], v_aug[:, par, t, :, 0:VA],
                                      start=(t == 0), stop=(t == NT - 1))
                        last.then_inc(s["w_kv"], 1)
                    if u_ == 4 and exists(it):
                        pe.wait_ge(s["kv_ready"], it + 1)
                        wait(pe, s["part_ready"], PARTS * (it + 1) + 1 if exists(it + 1) else 0)
                        for t in range(NT):
                            last = nc.tensor.transpose(work_ps[:, t * P:(t + 1) * P], feat[:, t, 0, :], ident[:])
                        last.then_inc(s["w_qfT"], 1)
                    if u_ == 6 and exists(it + 2):
                        pe.wait_ge(s["xn_ready"], NT * (it + 3))
                        wait(pe, s["v_copied"], it + 2)
                        wait(pe, s["xT_copied"], it + 3)
                        for t in range(NT):
                            last = nc.tensor.transpose(work_ps[:, t * P:(t + 1) * P], xn[:, t, :], ident[:])
                        last.then_inc(s["w_xT"], 1)
                    if u_ == 7 and exists(it + 2):
                        pe.wait_ge(s["xT_copied"], it + 4)
                        if isinstance(it, int) and it == -2:
                            pe.wait_ge(s["setup_v"], 1)
                        for t in range(NT):
                            dst = work_ps[:, t * 2 * C:(t + 1) * 2 * C]
                            mm(dst, xnT[:, par, t * P:(t + 1) * P], w_qk[:], start=True, stop=False)
                            last = mm(dst, ones_row[:], b_row[:, 0:2 * C], start=False, stop=True)
                        last.then_inc(s["w_qk_ready"], 1)

                for u_ in range(UNITS):
                    if exists(it if u_ >= 3 else it - 1):
                        turn(u_)
                    early(u_)
                    if u_ % 2 == 1 and exists(it if u_ >= 5 else it - 1):
                        product(u_)
                    if u_ in (4, 6) and exists(it - 1):
                        sums(u_)
                    late(u_)
                    if exists(it if u_ < UNITS - 1 else it + 1):
                        scores(u_)

            iterations(pe, body)


_NAMES = ["L0_attn_x", "L0_attn_Wqkv", "L0_attn_bqkv", "L0_attn_q_gamma", "L0_attn_q_beta", "L0_attn_k_gamma",
          "L0_attn_k_beta", "L0_attn_alpha", "L0_attn_Wproj", "L0_attn_bproj", "L0_ffn_W", "L0_ffn_b",
          "L0_ffn_logits", "L0_ffn_u"]


def kernel(**inputs):
    import concourse.bacc as bacc
    from concourse.bass_utils import run_bass_kernel_spmd

    nc = bacc.Bacc("TRN2", target_bir_lowering=False, num_devices=1)
    arrays, args = {}, []
    for name in _NAMES:
        a = np.ascontiguousarray(inputs[name])
        arrays[f"in_{name}"] = a
        args.append(nc.dram_tensor(f"in_{name}", a.shape, mybir.dt.from_np(a.dtype), kind="ExternalInput").ap())
    shape = arrays["in_L0_attn_x"].shape
    args.append(nc.dram_tensor("out_y", shape, F32, kind="ExternalOutput").ap())
    build(nc, *args)
    result = run_bass_kernel_spmd(nc, [arrays], core_ids=[0])
    return result.results[0]["out_y"]
```

```python
from contextlib import ExitStack

import numpy as np

import concourse.bass as bass
from concourse import mybir

F32 = mybir.dt.float32
BF16 = mybir.dt.bfloat16
ALU = mybir.AluOpType
ACT = mybir.ActivationFunctionType
AX_X = mybir.AxisListType.X

P = 128
H = 16
D = 8
C = H * D
N = 256
NT = N // P
TOPK = max(1, int(N * 0.05))
LN_EPS = 1e-5
SUM_EPS = 1e-8
SHARE_MIN = 1e-20
Z_EPS = 1e-6
SCORE_SCALE = float(1.0 / np.sqrt(np.float32(D)))
UNITS = H // 2
TILES = 4
QUADS = H // 4
VW = 32
VA = D + 1
REMOVED = -1.0
HUGE = float(2 ** 40)
PARTS = 3
SLOTS = [(0, 0), (0, 1), (0, 2), (1, 0), (1, 1), (1, 2), (2, 0), (2, 1)]
SLOTS_OF = ((slice(0, 3), slice(3, 6), slice(6, 8)), (slice(0, 8, 3), slice(1, 8, 3), slice(2, 8, 3)))
ROWS = len(SLOTS) * D
POOL_TILES = 3
RING = 8
FIRST = 4
X_STEPS = 5
QK_STEPS = 3


def wait(engine, semaphore, value):
    if isinstance(value, int) and value <= 0:
        return None
    return engine.wait_ge(semaphore, value)


def wait_alone(engine, semaphore, value, passed):
    w = wait(engine, semaphore, value)
    if w is not None:
        w.then_inc(passed, 1)


def build(nc, x, Wqkv, bqkv, q_gamma, q_beta, k_gamma, k_beta, alpha, Wproj, bproj, W, bW, logits, u, y):
    B = x.shape[0]
    OPS = W.shape[0]
    assert x.shape[1:] == (N, C) and 2 * ROWS == P
    for side in range(2):
        for p in range(PARTS):
            assert [parts[side] for parts in SLOTS[SLOTS_OF[side][p]]] == [p] * sum(parts[side] == p for parts in SLOTS)

    scratch = nc.dram_tensor("part_slots", (2, H * ROWS, N), BF16, kind="Internal").ap()
    x_t = x.rearrange("b (t p) c -> b p t c", p=P)
    y_t = y.rearrange("b (t p) c -> b p t c", p=P)

    def exists(batch):
        return not isinstance(batch, int) or 0 <= batch < B

    with ExitStack() as ctx:
        def sb(name, shape, dt=F32):
            return ctx.enter_context(nc.sbuf_tensor(name, shape, dt))

        def ps(name, shape, dt=F32):
            return ctx.enter_context(nc.psum_tensor(name, shape, dt))

        def sem(name):
            return ctx.enter_context(nc.semaphore(name))

        ident = sb("ident", [P, P])
        minus_huge = sb("minus_huge", [P, P], BF16)
        own_head = sb("own_head", [P, H, VA])
        ones_row = sb("ones_row", [1, P])
        eps_row = sb("eps_row", [1, H, VA])
        w_in = sb("w_in", [P, 4, P])
        w_qk = sb("w_qk", [P, 2 * C])
        w_v = sb("w_v", [P, C])
        w_proj = sb("w_proj", [P, C])
        w_mean = sb("w_mean", [P, 2 * H])
        b_row = sb("b_row", [1, 3 * C])
        b_mean = sb("b_mean", [1, 2 * H])
        b_out = sb("b_out", [1, C])
        w_ops = sb("w_ops", [P, OPS, C])
        b_ops = sb("b_ops", [1, OPS, C])
        w_sel = sb("w_sel", [P, C])
        b_sel = sb("b_sel", [1, C])
        gate = sb("gate", [P, 12, OPS])
        gamma_in = sb("gamma_in", [P, 2, D])
        beta_in = sb("beta_in", [P, 2, D])
        gamma = sb("gamma", [P, 2, H, D])
        beta = sb("beta", [P, 2, H, D])
        mix = sb("mix", [P, 7, H])

        x_sb = sb("x_sb", [P, 2, NT, C])
        stats = sb("stats", [P, NT, 6])
        x_mv = sb("x_mv", [P, NT, 2])
        x_ln = sb("x_ln", [P, NT])
        x_shift = sb("x_shift", [P, 2, NT])
        x_rsqrt = sb("x_rsqrt", [P, 4, NT])
        xn = sb("xn", [P, NT, C])
        xnT = sb("xnT", [P, 2, N])
        qk_sq = sb("qk_sq", [P, NT * 2 * C])
        qk_raw = sb("qk_raw", [P, NT * 2 * C])
        sq_half = sb("sq_half", [P, NT * 2 * H, 4])
        sq_quarter = sb("sq_quarter", [P, NT * 2 * H, 2])
        qk_ss = sb("qk_ss", [P, NT * 2 * H])
        qk_ln = sb("qk_ln", [P, NT * 2 * H])
        qk_rsqrt = sb("qk_rsqrt", [P, 4, NT * 2 * H])
        qk_a = sb("qk_a", [P, NT * 2 * C])
        qk_b = sb("qk_b", [P, NT * 2 * C])
        qkn = sb("qkn", [P, NT * 2 * C])
        qkT = sb("qkT", [P, 2, N])
        residue = sb("residue", [P, 2, 2, N])
        part = sb("part", [P, PARTS, 2, N], BF16)
        q_slots = sb("q_slots", [P, 2, UNITS, N], BF16)
        k_slots = sb("k_slots", [P, 2, UNITS, N], BF16)
        d_max = sb("d_max", [P, NT * 2 * H])
        d_sub = sb("d_sub", [P, NT * 2 * C])
        q_exp = sb("q_exp", [P, 2, NT, C])
        k_exp = sb("k_exp", [P, NT, C])
        k_sum = sb("k_sum", [P, NT * H])
        k_rec = sb("k_rec", [P, NT * H])
        k_feat = sb("k_feat", [P, NT, C])
        v_aug = sb("v_aug", [P, 2, NT, H, VW])
        kv = sb("kv", [P, H, VA])
        qfT = sb("qfT", [P, N])
        lin_z = sb("lin_z", [P, NT, H])
        lin = sb("lin", [P, 2, NT, C])
        ffn = sb("ffn", [P, NT, C])
        x_res = sb("x_res", [P, NT, C])
        base = sb("base", [P, 2, NT, C])

        top = sb("top", [P, 2, TILES, 9])
        drop = sb("drop", [P, 2, TILES, 9])
        e8 = sb("e8", [P, 2, TILES, 8])
        next8 = sb("next8", [P, RING, TILES, 8])
        rest = sb("rest", [P, TILES, N])
        e = sb("e", [P, RING, TILES, N])
        below = sb("below", [P, RING, TILES, N], BF16)
        kept = sb("kept", [P, 4, 2, NT, N])
        z = sb("z", [P, 2, NT, H])

        oT = sb("oT", [P, 2, QUADS, N])
        den = sb("den", [P, 2, NT, H])
        o_sparse = sb("o_sparse", [P, NT, C])
        o_sum = sb("o_sum", [P, NT, C])
        osT = sb("osT", [P, N])
        proj = sb("proj", [P, NT, C])
        out_sb = sb("out_sb", [P, NT, C])

        score_ps = ps("score_ps", [P, 2, 2, NT, N])
        turn_ps = ps("turn_ps", [P, 2, NT, N])
        pv_ps = ps("pv_ps", [P, 512])
        work_ps = ps("work_ps", [P, 512])

        names = """const_loaded w_loaded gate_loaded even_x_loaded odd_x_loaded res_loaded y_stored pool_const pool_step ident_ready setup_v setup_a setup_p gate_step shares_ready
            scores_ready top_ready rest_ready next_ready drop_ready e8_ready waits_passed
            exp_done below_pool below_act turn_ready turn_copied pv_ready pv_copied
            x_stats x_mean x_rsqrt_step x_rsqrt_ready x_newton xn_ready
            w_xT xT_copied w_qk_ready sq_ready sq_step raw_ready ss_ready qk_rsqrt_step qk_rsqrt_ready qk_newton
            n_step qkn_ready w_qkT qkT_copied part_ready residue_ready slots_written first_loaded slots_loaded
            dmax_ready dsub_ready dexp_ready ksum_ready krec_ready feat_ready
            w_v_ready v_copied w_kv kv_ready w_qfT qfT_copied w_lin linz_step lin_ready
            w_ffn ffn_copied base_ready
            w_turn den_step osp_ready osum_ready w_osT osT_copied w_proj_ready proj_copied
            y_ready""".split()
        s = {n: sem(n) for n in names}
        x_loaded = (s["even_x_loaded"], s["odd_x_loaded"])

        block = ctx.enter_context(nc.Block())

        def iterations(engine, body):
            first, last = 4, B - 2
            for it in range(-2, first):
                body(it, it % 2)
            with engine.Fori(first, last - 1, 2) as i:
                body(i, 0)
                body(i + 1, 1)
            for it in range(last, B + 2):
                body(it, it % 2)
        assert B % 2 == 0 and B >= 8

        @block.sync
        def _(sp):
            sp.dma_start(x_sb[:, 0], x_t[0]).then_inc(x_loaded[0], 16)
            for i, src in enumerate((Wqkv[0:P], Wqkv[P:2 * P], Wqkv[2 * P:3 * P], Wproj)):
                sp.dma_start(w_in[:, i, :], src).then_inc(s["w_loaded"], 16)
            sp.dma_start(b_row[:, :], bqkv.rearrange("(o c) -> o c", o=1)).then_inc(s["const_loaded"], 16)
            sp.dma_start(b_out[:, :], bproj.rearrange("(o c) -> o c", o=1)).then_inc(s["gate_loaded"], 16)
            for i, (g_in, b_in) in enumerate(((q_gamma, q_beta), (k_gamma, k_beta))):
                sp.dma_start(gamma_in[:, i, :], g_in.partition_broadcast(P)).then_inc(s["const_loaded"], 16)
                sp.dma_start(beta_in[:, i, :], b_in.partition_broadcast(P)).then_inc(s["const_loaded"], 16)
            sp.dma_start(x_sb[:, 1], x_t[1]).then_inc(x_loaded[1], 16)
            sp.dma_start(mix[:, 0, :], alpha.partition_broadcast(P)).then_inc(s["gate_loaded"], 16)
            sp.dma_start(gate[:, 0, :], logits.partition_broadcast(P)).then_inc(s["gate_loaded"], 16)
            sp.dma_start(gate[:, 1, :], u.partition_broadcast(P)).then_inc(s["gate_loaded"], 16)
            sp.dma_start(w_ops[:, :, :], W.rearrange("o d e -> d o e")).then_inc(s["gate_loaded"], 16)
            sp.dma_start(b_ops[:, :, :], bW.rearrange("(a o) e -> a o e", a=1)).then_inc(s["gate_loaded"], 16)

            def store(it):
                if exists(it - 2):
                    wait_alone(sp, s["y_ready"], it - 1, s["waits_passed"])
                    sp.dma_start(y_t[it - 2], out_sb[:]).then_inc(s["y_stored"], 16)

            def body(it, par):
                nxt = 1 - par
                if exists(it + 2) and not (isinstance(it, int) and it < 0):
                    wait_alone(sp, s["xn_ready"], NT * (it + 1), s["waits_passed"])
                    sp.dma_start(x_sb[:, par], x_t[it + 2]).then_inc(x_loaded[par], 16)
                if exists(it):
                    wait_alone(sp, s["base_ready"], it, s["waits_passed"])
                    sp.dma_start(x_res[:], x_t[it]).then_inc(s["res_loaded"], 16)
                if exists(it + 1):
                    wait_alone(sp, s["first_loaded"], 32 * (it + 1), s["waits_passed"])
                    wait_alone(sp, s["slots_loaded"], 32 * (it + 1), s["waits_passed"])
                    for p in range(PARTS):
                        wait_alone(sp, s["part_ready"], PARTS * (it + 1) + p + 1, s["waits_passed"])
                        for side in range(2):
                            slots = SLOTS_OF[side][p]
                            n = len(range(len(SLOTS))[slots])
                            dst = scratch[side].rearrange("(c s) n -> c s n", c=C)[:, slots]
                            sp.dma_start(dst, part[:, p, side, :].unsqueeze(1).to_broadcast([P, n, N])).then_inc(
                                s["slots_written"], 16)
                    wait_alone(sp, s["slots_written"], 16 * 2 * PARTS * (it + 2), s["waits_passed"])
                    wait_alone(sp, s["scores_ready"], UNITS * it, s["waits_passed"])
                    for units, loaded in ((slice(0, FIRST), "first_loaded"), (slice(FIRST, UNITS), "slots_loaded")):
                        for side, dst in enumerate((q_slots, k_slots)):
                            sp.dma_start(dst[:, nxt, units],
                                         scratch[side].rearrange("(g p) n -> p g n", p=P)[:, units]).then_inc(
                                             s[loaded], 16)
                store(it)

            iterations(sp, body)
            sp.wait_ge(s["y_stored"], 16 * B)

        @block.gpsimd
        def _(pool):
            def select(out, op, fill, base_, pattern, mult, n):
                pool.wait_ge(s["pool_step"], n)
                return nc.gpsimd.affine_select(out=out, in_=out, compare_op=op, fill=fill, base=base_,
                                               pattern=pattern, channel_multiplier=mult)
            nc.gpsimd.memset(ident[:], 0.0).then_inc(s["pool_step"], 1)
            select(ident[:], ALU.not_equal, 1.0, 0, [[-1, P]], 1, 1).then_inc(s["ident_ready"], 1)
            nc.gpsimd.memset(minus_huge[:], 0.0).then_inc(s["pool_step"], 1)
            nc.gpsimd.memset(own_head[:], 1.0).then_inc(s["pool_step"], 1)
            nc.gpsimd.memset(ones_row[:], 1.0).then_inc(s["pool_const"], 1)
            nc.gpsimd.memset(v_aug[:], 0.0).then_inc(s["pool_step"], 1)
            select(minus_huge[:], ALU.not_equal, -HUGE, 0, [[-1, P]], 1, 4).then_inc(s["pool_const"], 1)
            select(own_head[:], ALU.is_ge, 0.0, 0, [[-D, H], [0, VA]], 1, 4).then_inc(s["pool_step"], 1)
            select(own_head[:], ALU.is_ge, 0.0, D - 1, [[D, H], [0, VA]], -1, 5).then_inc(s["pool_const"], 1)
            for par in range(2):
                nc.gpsimd.memset(v_aug[:, par, :, :, D:VA], 1.0).then_inc(s["pool_const"], 1)
            nc.gpsimd.memset(top[:], 0.0).then_inc(s["pool_const"], 1)
            nc.gpsimd.memset(eps_row[:], 0.0).then_inc(s["pool_step"], 1)
            pool.wait_ge(s["pool_step"], 6)
            nc.gpsimd.memset(eps_row[:, :, D:VA], Z_EPS).then_inc(s["pool_const"], 1)
            gb = gamma[:].rearrange("p a h d -> p (a h d)")
            bb = beta[:].rearrange("p a h d -> p (a h d)")

            def halves(ap):
                return ap.rearrange("p (t f) -> p t f", t=NT)

            def heads(ap):
                return ap.rearrange("p (g d) -> p g d", d=D)

            def spread(ap):
                return ap.unsqueeze(2).to_broadcast([P, NT * 2 * H, D])

            def refine(rsqrt, kind, n):
                v, r, half, out = (rsqrt[:, i] for i in range(4))
                nc.gpsimd.tensor_tensor(half, half, v, ALU.mult).then_inc(s[kind + "_newton"], 1)
                wait_alone(pool, s[kind + "_newton"], n + 1, s["waits_passed"])
                nc.gpsimd.tensor_scalar(half, half, -1.0, 1.5, ALU.mult, ALU.add).then_inc(s[kind + "_newton"], 1)
                pool.wait_ge(s[kind + "_newton"], n + 2)
                nc.gpsimd.tensor_tensor(out, r, half, ALU.mult).then_inc(s[kind + "_newton"], 1)

            def normalise(it, n):
                if n == 0:
                    pool.wait_ge(s["raw_ready"], it + 2)
                    pool.wait_ge(s["qk_rsqrt_ready"], 2 * (it + 2))
                    refine(qk_rsqrt, "qk", QK_STEPS * (it + 1))
                    pool.wait_ge(s["qk_newton"], QK_STEPS * (it + 2))
                    nc.gpsimd.tensor_tensor(heads(qk_a[:]), heads(qk_raw[:]), spread(qk_rsqrt[:, 3]),
                                            ALU.mult).then_inc(s["n_step"], 1)
                else:
                    pool.wait_ge(s["n_step"], 2 * (it + 1) + n)
                    if isinstance(it, int) and it == -1:
                        pool.wait_ge(s["setup_v"], 5)
                    dst, src, other, op, done = (
                        (qk_b, qk_a, gb, ALU.mult, "n_step"), (qkn, qk_b, bb, ALU.add, "qkn_ready"))[n - 1]
                    nc.gpsimd.tensor_tensor(halves(dst[:]), halves(src[:]),
                                            other.unsqueeze(1).to_broadcast([P, NT, 2 * C]),
                                            op).then_inc(s[done], 1)

            def leave(it, p):
                pool.wait_ge(s["part_ready"], PARTS * (it + 1) + p + 1)
                if p == 0:
                    pool.wait_ge(s["qkT_copied"], it + 2)
                else:
                    pool.wait_ge(s["residue_ready"], 2 * (it + 1) + 1)
                src = qkT[:] if p == 0 else residue[:, 0]
                nc.gpsimd.tensor_tensor(residue[:, p], src, part[:, p], ALU.subtract).then_inc(s["residue_ready"], 1)

            def body(it, par):
                nxt = 1 - par
                for u_ in range(UNITS):
                    g = it * UNITS + u_
                    if u_ == 0 and exists(it + 1):
                        pool.wait_ge(s["sq_ready"], it + 2)
                        src = qk_sq[:].rearrange("p (g d) -> p g d", d=D)
                        for i, (dst, w) in enumerate(((sq_half[:], 4), (sq_quarter[:], 2),
                                                      (qk_ss[:].unsqueeze(2), 1))):
                            if i:
                                pool.wait_ge(s["sq_step"], 2 * (it + 1) + i)
                            nc.gpsimd.tensor_tensor(dst, src[:, :, 0:w], src[:, :, w:2 * w], ALU.add).then_inc(
                                s["sq_step" if i < 2 else "ss_ready"], 1)
                            src = dst
                    if u_ == 2 and exists(it + 1):
                        normalise(it, 1)
                    if u_ == 3 and exists(it + 1):
                        normalise(it, 2)
                    if u_ == 4 and exists(it + 1):
                        leave(it, 0)
                    if u_ == 5 and exists(it + 1):
                        leave(it, 1)
                    if exists(it if u_ >= 2 else it - 1):
                        r = (u_ - 2) % RING
                        for t in range(POOL_TILES):
                            wait_alone(pool, s["next_ready"], TILES * (g - 2) + t + 1, s["waits_passed"])
                            nc.gpsimd.tensor_scalar(below[:, r, t, :], e[:, r, t, :],
                                                    next8[:, r, t, TOPK - 9:TOPK - 8], None,
                                                    ALU.is_lt).then_inc(s["below_pool"], 1)
                    if u_ == 1 and exists(it + 1):
                        normalise(it, 0)
                    if u_ == 0 and exists(it - 2):
                        pool.wait_ge(s["osp_ready"], NT * (it - 1))
                        pool.wait_ge(s["lin_ready"], it - 1)
                        nc.gpsimd.tensor_tensor(o_sum[:], o_sparse[:], lin[:, par],
                                                ALU.add).then_inc(s["osum_ready"], 1)
                    if u_ == 3 and exists(it + 1):
                        pool.wait_ge(s["dmax_ready"], it + 2)
                        nc.gpsimd.tensor_tensor(heads(d_sub[:]), heads(qkn[:]), spread(d_max[:]),
                                                ALU.subtract).then_inc(s["dsub_ready"], 1)
                    if u_ == 4 and exists(it + 2):
                        pool.wait_ge(s["x_rsqrt_ready"], 2 * (it + 3))
                        n = X_STEPS * (it + 2)
                        refine(x_rsqrt, "x", n)
                        pool.wait_ge(s["x_newton"], n + 3)
                        nc.gpsimd.tensor_tensor(x_shift[:, 0], x_mv[:, :, 0], x_rsqrt[:, 3],
                                                ALU.mult).then_inc(s["x_newton"], 1)
                        wait_alone(pool, s["x_newton"], n + 4, s["waits_passed"])
                        nc.gpsimd.tensor_scalar(x_shift[:, 1], x_shift[:, 0], -1.0, None,
                                                ALU.mult).then_inc(s["x_newton"], 1)
                    if u_ == 6 and exists(it - 2):
                        pool.wait_ge(s["proj_copied"], it - 1)
                        wait(pool, s["y_stored"], 16 * (it - 2))
                        nc.gpsimd.tensor_tensor(out_sb[:], proj[:], base[:, par], ALU.add).then_inc(s["y_ready"], 1)
                    if u_ == 6 and exists(it):
                        pool.wait_ge(s["ffn_copied"], it + 1)
                        pool.wait_ge(s["res_loaded"], 16 * (it + 1))
                        wait(pool, s["y_ready"], it - 1)
                        nc.gpsimd.tensor_tensor(base[:, par], ffn[:], x_res[:],
                                                ALU.add).then_inc(s["base_ready"], 1)
                    if u_ == 7 and exists(it + 1):
                        pool.wait_ge(s["krec_ready"], it + 2)
                        pool.wait_ge(s["dexp_ready"], 2 * (it + 2))
                        nc.gpsimd.tensor_tensor(k_feat[:].rearrange("p t (h d) -> p (t h) d", d=D),
                                                k_exp[:].rearrange("p t (h d) -> p (t h) d", d=D),
                                                k_rec[:].unsqueeze(2).to_broadcast([P, NT * H, D]),
                                                ALU.mult).then_inc(s["feat_ready"], 1)

            iterations(pool, body)

        @block.vector
        def _(dve):
            step = [0]

            def setup(ins):
                step[0] += 1
                ins.then_inc(s["setup_p"], 1)
                dve.wait_ge(s["setup_p"], step[0])

            def stage_weights():
                dve.wait_ge(s["setup_a"], 1)
                wq4 = w_qk[:].rearrange("p (g d) -> p g d", d=D)
                setup(nc.vector.tensor_reduce(w_mean[:], wq4, AX_X, ALU.add))
                setup(nc.vector.tensor_scalar(w_mean[:], w_mean[:], 1.0 / D, None, ALU.mult))
                setup(nc.vector.tensor_tensor(wq4, wq4, w_mean[:].unsqueeze(2).to_broadcast([P, 2 * H, D]), ALU.subtract))
                dve.wait_ge(s["const_loaded"], 16 * 5)
                bq4 = b_row[:, 0:2 * C].rearrange("p (g d) -> p g d", d=D)
                setup(nc.vector.tensor_reduce(b_mean[:], bq4, AX_X, ALU.add))
                setup(nc.vector.tensor_scalar(b_mean[:], b_mean[:], 1.0 / D, None, ALU.mult))
                nc.vector.tensor_tensor(bq4, bq4, b_mean[:].unsqueeze(2).to_broadcast([1, 2 * H, D]),
                                        ALU.subtract).then_inc(s["setup_v"], 1)
                dve.wait_ge(s["setup_v"], 1)
                for i, factor in enumerate((SCORE_SCALE, 1.0)):
                    for dst, src in ((gamma, gamma_in), (beta, beta_in)):
                        nc.vector.tensor_scalar(dst[:, i], src[:, i].unsqueeze(1).to_broadcast([P, H, D]), factor, None,
                                                ALU.mult).then_inc(s["setup_v"], 1)

            def stage_gate():
                dve.wait_ge(s["gate_loaded"], 16 * 6)
                dve.wait_ge(s["pool_const"], 7)
                setup(nc.vector.reduce_max(gate[:, 2, 0:1], gate[:, 0, :], AX_X))
                nc.vector.tensor_scalar(gate[:, 3, :], gate[:, 0, :], gate[:, 2, 0:1], None,
                                        ALU.subtract).then_inc(s["setup_v"], 1)
                for i in range(OPS):
                    last = nc.vector.memset(gate[:, 4, i:i + 1], float(OPS - i))
                setup(last)
                dve.wait_ge(s["setup_a"], 2)
                dve.wait_ge(s["setup_v"], 6)
                setup(nc.vector.tensor_scalar(mix[:, 1, :], mix[:, 1, :], 1.0, None, ALU.add))
                setup(nc.vector.reciprocal(mix[:, 2, :], mix[:, 1, :]))
                setup(nc.vector.tensor_scalar(mix[:, 3, :], mix[:, 2, :], SHARE_MIN, None, ALU.max))
                setup(nc.vector.tensor_scalar(mix[:, 4, :], mix[:, 2, :], -1.0, 1.0, ALU.mult, ALU.add))
                setup(nc.vector.reciprocal(mix[:, 5, :], mix[:, 3, :]))
                setup(nc.vector.tensor_tensor(mix[:, 6, :], mix[:, 4, :], mix[:, 5, :], ALU.mult))
                for part_, rows, cols in ((w_v[:], P, mix[:, 3, :]), (b_row[:, 2 * C:3 * C], 1, mix[0:1, 3, :])):
                    v4 = part_.rearrange("p (h d) -> p h d", d=D)
                    nc.vector.tensor_tensor(v4, v4, cols.unsqueeze(2).to_broadcast([rows, H, D]),
                                            ALU.mult).then_inc(s["shares_ready"], 1)
                nc.vector.tensor_tensor(own_head[:, :, 0:D], own_head[:, :, 0:D],
                                        mix[:, 6, :].unsqueeze(2).to_broadcast([P, H, D]),
                                        ALU.mult).then_inc(s["shares_ready"], 1)
                setup(nc.vector.tensor_scalar(gate[:, 3, :], gate[:, 3, :], gate[:, 5, 1:2], None, ALU.subtract))
                setup(nc.vector.tensor_tensor(gate[:, 3, :], gate[:, 3, :], gate[:, 6, :], ALU.subtract))
                setup(nc.vector.reduce_max(gate[:, 2, 1:2], gate[:, 3, :], AX_X))
                setup(nc.vector.scalar_tensor_tensor(out=gate[:, 7, :], in0=gate[:, 3, :], scalar=gate[:, 2, 1:2],
                                                     in1=gate[:, 4, :], op0=ALU.is_ge, op1=ALU.mult))
                setup(nc.vector.reduce_max(gate[:, 2, 2:3], gate[:, 7, :], AX_X))
                setup(nc.vector.tensor_scalar(gate[:, 8, :], gate[:, 7, :], gate[:, 2, 2:3], None, ALU.is_ge))
                for dst, src, one in ((w_sel, w_ops, gate), (b_sel, b_ops, gate[0:1])):
                    setup(nc.vector.tensor_scalar(dst[:], src[:, 0, :], one[:, 8, 0:1], None, ALU.mult))
                    for i in range(1, OPS):
                        setup(nc.vector.scalar_tensor_tensor(out=dst[:], in0=src[:, i, :], scalar=one[:, 8, i:i + 1],
                                                             in1=dst[:], op0=ALU.mult, op1=ALU.add))
                nc.vector.tensor_tensor(b_out[:], b_out[:], b_sel[:], ALU.add).then_inc(s["setup_v"], 1)
            def alone(semaphore, value):
                wait_alone(dve, semaphore, value, s["waits_passed"])

            def body(it, par):
                nxt = 1 - par

                def largest(g, q, t):
                    alone(s["scores_ready"], g + 1)
                    nc.vector.max(top[:, q, t, 1:9], score_ps[:, q, t // 2, t % 2, :]).then_inc(s["top_ready"], 1)

                def remove(u_, t):
                    g1 = it * UNITS + u_ - 1
                    wait(dve, s["next_ready"], TILES * (g1 - 1) + t + 1)
                    alone(s["e8_ready"], g1 + 1)
                    nc.vector.match_replace(rest[:, t, :], e8[:, (u_ - 1) % 2, t, :], e[:, (u_ - 1) % RING, t, :],
                                            REMOVED).then_inc(s["rest_ready"], 1)

                def following(u_, t):
                    alone(s["rest_ready"], TILES * (it * UNITS + u_ - 1) + t + 1)
                    nc.vector.max(next8[:, (u_ - 1) % RING, t, :], rest[:, t, :]).then_inc(s["next_ready"], 1)

                def extra(u_, k):
                    if u_ == 2 and k == 1 and exists(it):
                        if isinstance(it, int) and it == 0:
                            dve.wait_ge(s["shares_ready"], 3)
                        dve.wait_ge(s["w_kv"], it + 1)
                        nc.vector.tensor_tensor(kv[:], work_ps[:, 0:H * VA].rearrange("p (h e) -> p h e", e=VA),
                                                own_head[:], ALU.mult).then_inc(s["kv_ready"], 1)
                    if u_ == 5 and 3 <= k <= 5 and exists(it):
                        w = work_ps[:, 0:NT * H * VA].rearrange("p (t h e) -> p t h e", t=NT, e=VA)
                        if k == 3:
                            dve.wait_ge(s["w_lin"], it + 1)
                            nc.vector.reciprocal(lin_z[:], w[:, :, :, D]).then_inc(s["linz_step"], 1)
                        if k == 5:
                            dve.wait_ge(s["linz_step"], it + 1)
                            nc.vector.tensor_tensor(
                                lin[:, par].rearrange("p t (h d) -> p (t h) d", d=D),
                                work_ps[:, 0:NT * H * VA].rearrange("p (g e) -> p g e", e=VA)[:, :, 0:D],
                                lin_z[:].rearrange("p t h -> p (t h)").unsqueeze(2).to_broadcast([P, NT * H, D]),
                                ALU.mult).then_inc(s["lin_ready"], 1)
                    if u_ == 3 and k == 5 and exists(it + 1):
                        dve.wait_ge(s["qkn_ready"], it + 2)
                        nc.vector.tensor_reduce(d_max[:], qkn[:].rearrange("p (g d) -> p g d", d=D), AX_X,
                                                ALU.max).then_inc(s["dmax_ready"], 1)
                    if u_ in (5, 7) and 1 <= k <= 4 and exists(it - 1):
                        t = (u_ - 5) // 2
                        w = pv_ps[:].rearrange("p (h e) -> p h e", e=VW)
                        n = 2 * (NT * (it - 1) + t)
                        if k == 1:
                            dve.wait_ge(s["w_turn"], NT * (it - 1) + t + 1)
                            nc.vector.scalar_tensor_tensor(out=den[:, 0, t], in0=z[:, nxt, t], scalar=SUM_EPS,
                                                           in1=w[:, :, D], op0=ALU.mult,
                                                           op1=ALU.add).then_inc(s["den_step"], 1)
                        if k == 2:
                            dve.wait_ge(s["den_step"], n + 1)
                            nc.vector.reciprocal(den[:, 1, t], den[:, 0, t]).then_inc(s["den_step"], 1)
                        if k == 4:
                            dve.wait_ge(s["den_step"], n + 2)
                            nc.vector.tensor_tensor(o_sparse[:, t].rearrange("p (h d) -> p h d", d=D), w[:, :, 0:D],
                                                    den[:, 1, t].unsqueeze(2).to_broadcast([P, H, D]),
                                                    ALU.mult).then_inc(s["osp_ready"], 1)
                    if u_ == 1 and exists(it + 2):
                        if k == 0:
                            dve.wait_ge(x_loaded[par], 16 + 8 * (it + 2 - par))
                            for t in range(NT):
                                nc.vector.bn_stats(stats[:, t], x_sb[:, par, t]).then_inc(s["x_stats"], 1)
                        if k == 5:
                            alone(s["x_stats"], NT * (it + 3))
                            alone(s["x_newton"], X_STEPS * (it + 2))
                            for t in range(NT):
                                nc.vector.bn_aggr(x_mv[:, t], stats[:, t]).then_inc(s["x_mean"], 1)
                    if u_ == 5 and exists(it + 1):
                        if k == 5:
                            dve.wait_ge(s["dexp_ready"], 2 * (it + 2))
                            nc.vector.tensor_reduce(k_sum[:], k_exp[:].rearrange("p t (h d) -> p (t h) d", d=D), AX_X,
                                                    ALU.add).then_inc(s["ksum_ready"], 1)
                    if u_ == 6 and exists(it + 1) and k == 5:
                        dve.wait_ge(s["ksum_ready"], it + 2)
                        nc.vector.reciprocal(k_rec[:], k_sum[:]).then_inc(s["krec_ready"], 1)

                for u_ in range(UNITS):
                    if isinstance(it, int) and (it, u_) == (-2, 2):
                        stage_weights()
                    if isinstance(it, int) and (it, u_) == (-1, 2):
                        stage_gate()
                    g = it * UNITS + u_
                    q = u_ % 2
                    before = exists(it if u_ else it - 1)
                    if exists(it):
                        for t in range(TILES):
                            largest(g, q, t)
                    if before:
                        remove(u_, 0)
                    if exists(it):
                        dve.wait_ge(s["top_ready"], TILES * (g + 1))
                        nc.vector.tensor_tensor(drop[:, q], top[:, q], top[:, q, :, 1:2].to_broadcast(
                            [P, TILES, 9]), ALU.subtract).then_inc(s["drop_ready"], 1)
                    extra(u_, 0)
                    if before:
                        remove(u_, 1)
                    extra(u_, 1)
                    if before:
                        following(u_, 0)
                    extra(u_, 2)
                    if before:
                        remove(u_, 2)
                    extra(u_, 3)
                    if before:
                        following(u_, 1)
                    extra(u_, 4)
                    if before:
                        remove(u_, 3)
                        following(u_, 2)
                    extra(u_, 5)
                    if before:
                        following(u_, 3)

            iterations(dve, body)

        @block.scalar
        def _(act):
            nc.scalar.preload_act_table_set("natural_log_exp_and_others")
            act.wait_ge(s["w_xT"], 1)
            nc.scalar.copy(w_qk[:], work_ps[:, 0:2 * C]).then_inc(s["setup_a"], 1)
            nc.scalar.copy(w_v[:], work_ps[:, 2 * C:3 * C])
            nc.scalar.copy(w_proj[:], work_ps[:, 3 * C:4 * C]).then_inc(s["xT_copied"], 1)

            def stage_gate():
                act.wait_ge(s["setup_v"], 6)
                nc.scalar.activation(gate[:, 9, :], gate[:, 3, :], ACT.Exp,
                                     accum_out=gate[:, 5, 0:1]).then_inc(s["gate_step"], 1)
                nc.scalar.activation(gate[:, 10, :], gate[:, 1, :], ACT.Ln).then_inc(s["gate_step"], 1)
                nc.scalar.activation(mix[:, 1, :], mix[:, 0, :], ACT.Exp, scale=-1.0).then_inc(s["gate_step"], 1)
                act.wait_ge(s["gate_step"], 3)
                nc.scalar.activation(gate[:, 5, 1:2], gate[:, 5, 0:1], ACT.Ln)
                nc.scalar.activation(gate[:, 6, :], gate[:, 10, :], ACT.Ln, scale=-1.0).then_inc(s["setup_a"], 1)

            def rsqrt_steps(rsqrt, log, src, scale, kind, n):
                wait(act, s[kind + "_newton"], (X_STEPS if kind == "x" else QK_STEPS) * n)
                nc.scalar.activation(log, src, ACT.Ln, scale=scale, bias=LN_EPS).then_inc(s[kind + "_rsqrt_step"], 1)
                nc.scalar.activation(rsqrt[:, 0], src, ACT.Identity, scale=scale, bias=LN_EPS).then_inc(
                    s[kind + "_rsqrt_ready"], 1)
                act.wait_ge(s[kind + "_rsqrt_step"], 2 * n + 1)
                nc.scalar.activation(rsqrt[:, 1], log, ACT.Exp, scale=-0.5).then_inc(s[kind + "_rsqrt_step"], 1)
                act.wait_ge(s[kind + "_rsqrt_step"], 2 * n + 2)
                nc.scalar.activation(rsqrt[:, 2], rsqrt[:, 1], ACT.Square, scale=float(0.5 ** 0.5)).then_inc(
                    s[kind + "_rsqrt_ready"], 1)

            def body(it, par):
                nxt = 1 - par
                for u_ in range(UNITS):
                    if isinstance(it, int) and (it, u_) == (-2, 7):
                        stage_gate()
                    g = it * UNITS + u_
                    if exists(it if u_ >= 4 else it - 1):
                        wait(act, s["pv_ready"], it * QUADS + (u_ - 8) // 2 + 1)
                        for hh in range(2):
                            act.wait_ge(s["turn_ready"], 2 * (g - 4) + hh + 1)
                            nc.scalar.activation(kept[:, u_ % 4, hh], turn_ps[:, hh], ACT.Relu).then_inc(
                                s["turn_copied"], 1)

                    if u_ == 1 and exists(it - 2):
                        act.wait_ge(s["w_osT"], it - 1)
                        nc.scalar.copy(osT[:], work_ps[:, 0:N]).then_inc(s["osT_copied"], 1)
                    if u_ == 1 and exists(it + 1):
                        act.wait_ge(s["ss_ready"], it + 2)
                        rsqrt_steps(qk_rsqrt, qk_ln[:], qk_ss[:], 1.0 / D, "qk", it + 1)
                    if u_ == 4 and exists(it + 1):
                        act.wait_ge(s["w_qkT"], it + 2)
                        wait(act, s["residue_ready"], 2 * (it + 1))
                        nc.scalar.copy(qkT[:], work_ps[:].rearrange("p (a n) -> p a n", a=2)).then_inc(
                            s["qkT_copied"], 1)
                        wait(act, s["slots_written"], 16 * 2 * PARTS * (it + 1))
                        nc.scalar.copy(part[:, 0], work_ps[:].rearrange("p (a n) -> p a n", a=2)).then_inc(
                            s["part_ready"], 1)
                    if u_ == 6 and exists(it + 1):
                        act.wait_ge(s["w_v_ready"], it + 2)
                        nc.scalar.copy(v_aug[:, nxt, :, :, 0:D].rearrange("p t h d -> p (t h) d"),
                                       work_ps[:, 0:NT * C].rearrange("p (g d) -> p g d", d=D)).then_inc(
                                           s["v_copied"], 1)
                    if exists(it):
                        act.wait_ge(s["drop_ready"], g + 1)
                        if u_ == 0:
                            wait(act, s["osp_ready"], NT * (it - 1))
                        wait(act, s["turn_ready"], 2 * (g - RING + 1))
                        for t in range(TILES):
                            nc.scalar.activation(e[:, u_ % RING, t, :], score_ps[:, u_ % 2, t // 2, t % 2, :], ACT.Exp,
                                                 bias=drop[:, u_ % 2, t, 0:1],
                                                 accum_out=z[:, par, t % 2, 2 * u_ + t // 2:2 * u_ + t // 2 + 1]
                                                 ).then_inc(s["exp_done"], 1)
                        nc.scalar.activation(e8[:, u_ % 2], drop[:, u_ % 2, :, 1:9], ACT.Exp).then_inc(s["e8_ready"], 1)

                    if exists(it if u_ >= 2 else it - 1):
                        r = (u_ - 2) % RING
                        act.wait_ge(s["next_ready"], TILES * (g - 1))
                        for t in range(POOL_TILES, TILES):
                            nc.scalar.activation(below[:, r, t, :], e[:, r, t, :], ACT.Relu, scale=-1.0,
                                                 bias=next8[:, r, t, TOPK - 9:TOPK - 8]).then_inc(s["below_act"], 1)

                    if u_ % 2 == 0 and exists(it if u_ >= 6 else it - 1):
                        act.wait_ge(s["pv_ready"], it * QUADS + (u_ - 6) // 2 + 1)
                        if u_ == 6:
                            wait(act, s["w_turn"], NT * (it - 1))
                        nc.scalar.copy(oT[:, par if u_ >= 6 else nxt, (u_ - 6) // 2 % 4], pv_ps[:, 0:N]).then_inc(
                            s["pv_copied"], 1)

                    if u_ == 0 and exists(it):
                        act.wait_ge(s["w_ffn"], it + 1)
                        wait(act, s["base_ready"], it)
                        nc.scalar.copy(ffn[:], work_ps[:, 0:NT * C].rearrange("p (t c) -> p t c", t=NT)).then_inc(
                            s["ffn_copied"], 1)
                    if u_ == 4 and exists(it):
                        act.wait_ge(s["w_qfT"], it + 1)
                        nc.scalar.copy(qfT[:], work_ps[:, 0:N]).then_inc(s["qfT_copied"], 1)
                    if u_ in (4, 5) and exists(it + 1):
                        p = u_ - 3
                        act.wait_ge(s["residue_ready"], 2 * (it + 1) + p)
                        nc.scalar.copy(part[:, p], residue[:, p - 1]).then_inc(s["part_ready"], 1)
                    if u_ == 4 and exists(it + 1):
                        act.wait_ge(s["dsub_ready"], it + 2)
                        sub = d_sub[:].rearrange("p (t a c) -> p t a c", t=NT, a=2)
                        for side, dst, factor in ((0, q_exp[:, nxt], 1.0 / SCORE_SCALE), (1, k_exp[:], 1.0)):
                            nc.scalar.activation(dst, sub[:, :, side, :], ACT.Exp,
                                                 scale=factor).then_inc(s["dexp_ready"], 1)
                    if u_ == 2 and exists(it - 2):
                        act.wait_ge(s["w_proj_ready"], it - 1)
                        wait(act, s["y_ready"], it - 2)
                        nc.scalar.copy(proj[:], work_ps[:, 0:NT * C].rearrange("p (t c) -> p t c", t=NT)).then_inc(
                            s["proj_copied"], 1)
                    if u_ == 2 and exists(it + 2):
                        act.wait_ge(s["x_mean"], NT * (it + 3))
                        rsqrt_steps(x_rsqrt, x_ln[:], x_mv[:, :, 1], 1.0, "x", it + 2)
                    if u_ == 5 and exists(it + 2):
                        act.wait_ge(s["x_newton"], X_STEPS * (it + 3))
                        wait(act, s["w_xT"], it + 3)
                        for t in range(NT):
                            nc.scalar.activation(xn[:, t], x_sb[:, par, t], ACT.Identity, scale=x_rsqrt[:, 3, t:t + 1],
                                                 bias=x_shift[:, 1, t:t + 1]).then_inc(s["xn_ready"], 1)
                    if u_ == 6 and exists(it + 2):
                        act.wait_ge(s["w_xT"], it + 4)
                        nc.scalar.copy(xnT[:, par], work_ps[:, 0:N]).then_inc(s["xT_copied"], 1)
                    if u_ == 7 and exists(it + 2):
                        act.wait_ge(s["w_qk_ready"], it + 3)
                        nc.scalar.activation(qk_sq[:], work_ps[:], ACT.Square).then_inc(s["sq_ready"], 1)
                        wait(act, s["n_step"], 2 * (it + 2))
                        nc.scalar.copy(qk_raw[:], work_ps[:]).then_inc(s["raw_ready"], 1)

            iterations(act, body)

        @block.tensor
        def _(pe):
            mm = nc.tensor.matmul
            pe.wait_ge(s["w_loaded"], 16 * 4)
            pe.wait_ge(s["ident_ready"], 1)
            for i in range(4):
                last = nc.tensor.transpose(work_ps[:, i * P:(i + 1) * P], w_in[:, i, :], ident[:])
            last.then_inc(s["w_xT"], 1)

            def body(it, par):
                nxt = 1 - par

                def scores(u_):
                    g1 = it * UNITS + u_ + 1
                    side, v_ = (par, u_ + 1) if u_ < UNITS - 1 else (nxt, 0)
                    if v_ == 0:
                        pe.wait_ge(s["first_loaded"], 32 * (it + 2))
                    if v_ == FIRST:
                        pe.wait_ge(s["slots_loaded"], 32 * (it + 1))
                    wait_alone(pe, s["exp_done"], TILES * (g1 - 1), s["waits_passed"])
                    for t in range(TILES):
                        hh, nt = t // 2, t % 2
                        rows = slice(ROWS * hh, ROWS * (hh + 1))
                        last = mm(score_ps[:, v_ % 2, hh, nt, :], q_slots[rows, side, v_, nt * P:(nt + 1) * P],
                                  k_slots[rows, side, v_, :], start=True, stop=True)
                    last.then_inc(s["scores_ready"], 1)

                def turn(u_):
                    g2 = it * UNITS + u_ - 4
                    r = (u_ - 4) % RING
                    pe.wait_ge(s["below_pool"], POOL_TILES * (g2 + 1))
                    pe.wait_ge(s["below_act"], (TILES - POOL_TILES) * (g2 + 1))
                    for hh in range(2):
                        wait(pe, s["turn_copied"], 2 * (g2 - 1) + hh + 1)
                        for nt in range(NT):
                            t = 2 * hh + nt
                            for mc in range(NT):
                                dst = turn_ps[:, hh, mc, nt * P:(nt + 1) * P]
                                keys = slice(mc * P, (mc + 1) * P)
                                mm(dst, e[:, r, t, keys], ident[:], start=True, stop=False, is_transpose=True)
                                last = mm(dst, below[:, r, t, keys], minus_huge[:], start=False, stop=True)
                        last.then_inc(s["turn_ready"], 1)

                def product(u_):
                    quad = it * QUADS + (u_ - 6) // 2
                    side = par if u_ >= 6 else nxt
                    q = (u_ - 6) // 2 % 4
                    pe.wait_ge(s["turn_copied"], 4 * (quad + 1))
                    wait(pe, s["pv_copied"], quad)
                    if u_ in (0, 6):
                        wait(pe, s["osp_ready"], NT * (it - 1) + (1 if u_ == 6 else 0))
                    for mc in range(NT):
                        for j in range(4):
                            v_ = 2 * q + j // 2
                            last = mm(pv_ps[32 * j:32 * (j + 1), 0:N], v_aug[:, side, mc, 4 * q + j, :],
                                      kept[:, v_ % 4, j % 2, mc, :], start=(mc == 0), stop=(mc == NT - 1),
                                      tile_position=(0, 32 * j))
                    last.then_inc(s["pv_ready"], 1)

                def sums(u_):
                    t = (u_ - 5) // 2
                    pe.wait_ge(s["pv_copied"], QUADS * it + (t if exists(it) else 0))
                    if t:
                        pe.wait_ge(s["osp_ready"], NT * (it - 1) + t)
                    for q in range(QUADS):
                        last = nc.tensor.transpose(pv_ps[:, q * P:(q + 1) * P],
                                                   oT[:, nxt, q, t * P:(t + 1) * P], ident[:])
                    last.then_inc(s["w_turn"], 1)

                def early(u_):
                    if u_ == 1 and exists(it - 2):
                        pe.wait_ge(s["osum_ready"], it - 1)
                        if exists(it):
                            pe.wait_ge(s["ffn_copied"], it + 1)
                        else:
                            pe.wait_ge(s["lin_ready"], B)
                            pe.wait_ge(s["proj_copied"], it - 2)
                        for t in range(NT):
                            last = nc.tensor.transpose(work_ps[:, t * P:(t + 1) * P], o_sum[:, t, :], ident[:])
                        last.then_inc(s["w_osT"], 1)
                    if u_ == 5 and exists(it):
                        pe.wait_ge(s["qfT_copied"], it + 1)
                        for t in range(NT):
                            last = mm(work_ps[:, t * H * VA:(t + 1) * H * VA], qfT[:, t * P:(t + 1) * P],
                                      kv[:].rearrange("p h e -> p (h e)"), start=True, stop=True)
                        last.then_inc(s["w_lin"], 1)
                    if u_ == 6 and exists(it + 1):
                        if isinstance(it, int) and it == -1:
                            pe.wait_ge(s["shares_ready"], 3)
                        wait(pe, s["part_ready"], PARTS * (it + 1) + 1)
                        wait(pe, s["lin_ready"], it + 1)
                        for t in range(NT):
                            dst = work_ps[:, t * C:(t + 1) * C]
                            mm(dst, xnT[:, nxt, t * P:(t + 1) * P], w_v[:], start=True, stop=False)
                            last = mm(dst, ones_row[:], b_row[:, 2 * C:3 * C], start=False, stop=True)
                        last.then_inc(s["w_v_ready"], 1)
                    if u_ == 7 and exists(it + 2):
                        pe.wait_ge(s["xT_copied"], it + 4)
                        if isinstance(it, int) and it == -2:
                            pe.wait_ge(s["setup_v"], 1)
                            pe.wait_ge(s["pool_const"], 7)
                        for t in range(NT):
                            dst = work_ps[:, t * 2 * C:(t + 1) * 2 * C]
                            mm(dst, xnT[:, par, t * P:(t + 1) * P], w_qk[:], start=True, stop=False)
                            last = mm(dst, ones_row[:], b_row[:, 0:2 * C], start=False, stop=True)
                        last.then_inc(s["w_qk_ready"], 1)

                def late(u_):
                    if u_ == 0 and exists(it):
                        if exists(it + 1):
                            pe.wait_ge(s["raw_ready"], it + 2)
                        else:
                            pe.wait_ge(s["v_copied"], it + 1)
                        pe.wait_ge(s["setup_v"], 7)
                        for t in range(NT):
                            dst = work_ps[:, t * C:(t + 1) * C]
                            mm(dst, xnT[:, par, t * P:(t + 1) * P], w_sel[:], start=True, stop=False)
                            last = mm(dst, ones_row[:], b_out[:], start=False, stop=True)
                        last.then_inc(s["w_ffn"], 1)
                    if u_ == 1 and exists(it):
                        pe.wait_ge(s["ffn_copied"], it + 1)
                        wait(pe, s["osT_copied"], it - 1)
                        pe.wait_ge(s["feat_ready"], it + 1)
                        for t in range(NT):
                            mm(work_ps[:, 0:H * VA], k_feat[:, t, :], v_aug[:, par, t, :, 0:VA],
                               start=(t == 0), stop=False)
                        last = mm(work_ps[:, 0:H * VA], ones_row[:], eps_row[:].rearrange("o h e -> o (h e)"),
                                  start=False, stop=True)
                        last.then_inc(s["w_kv"], 1)
                    if u_ == 2 and exists(it - 2):
                        pe.wait_ge(s["osT_copied"], it - 1)
                        wait(pe, s["kv_ready"], it + 1 if exists(it) else 0)
                        for t in range(NT):
                            last = mm(work_ps[:, t * C:(t + 1) * C], osT[:, t * P:(t + 1) * P], w_proj[:],
                                      start=True, stop=True)
                        last.then_inc(s["w_proj_ready"], 1)
                    if u_ == 3 and exists(it + 1):
                        wait(pe, s["kv_ready"], it + 1)
                        wait(pe, s["proj_copied"], it - 1)
                        pe.wait_ge(s["qkn_ready"], it + 2)
                        for side in range(2):
                            for t in range(NT):
                                last = nc.tensor.transpose(
                                    work_ps[:, side * N + t * P:side * N + (t + 1) * P],
                                    qkn[:, (2 * t + side) * C:(2 * t + side + 1) * C], ident[:])
                        last.then_inc(s["w_qkT"], 1)
                    if u_ == 4 and exists(it):
                        pe.wait_ge(s["kv_ready"], it + 1)
                        pe.wait_ge(s["dexp_ready"], 2 * it + 1)
                        if exists(it + 1):
                            pe.wait_ge(s["part_ready"], PARTS * (it + 1) + 1)
                        else:
                            pe.wait_ge(s["proj_copied"], it - 1)
                        for t in range(NT):
                            last = nc.tensor.transpose(work_ps[:, t * P:(t + 1) * P], q_exp[:, par, t, :], ident[:])
                        last.then_inc(s["w_qfT"], 1)
                    if u_ == 6 and exists(it + 2):
                        pe.wait_ge(s["xn_ready"], NT * (it + 3))
                        wait(pe, s["v_copied"], it + 2)
                        wait(pe, s["xT_copied"], it + 3)
                        for t in range(NT):
                            last = nc.tensor.transpose(work_ps[:, t * P:(t + 1) * P], xn[:, t, :], ident[:])
                        last.then_inc(s["w_xT"], 1)

                for u_ in range(UNITS):
                    if exists(it if u_ >= 4 else it - 1):
                        turn(u_)
                    if u_ % 2 == 0 and exists(it if u_ >= 6 else it - 1):
                        product(u_)
                    if u_ in (5, 7) and exists(it - 1):
                        sums(u_)
                    early(u_)
                    if exists(it if u_ < UNITS - 1 else it + 1):
                        scores(u_)
                    late(u_)

            iterations(pe, body)


_NAMES = ["L0_attn_x", "L0_attn_Wqkv", "L0_attn_bqkv", "L0_attn_q_gamma", "L0_attn_q_beta", "L0_attn_k_gamma",
          "L0_attn_k_beta", "L0_attn_alpha", "L0_attn_Wproj", "L0_attn_bproj", "L0_ffn_W", "L0_ffn_b",
          "L0_ffn_logits", "L0_ffn_u"]


def kernel(**inputs):
    import concourse.bacc as bacc
    from concourse.bass_utils import run_bass_kernel_spmd

    nc = bacc.Bacc("TRN2", target_bir_lowering=False, num_devices=1)
    arrays, args = {}, []
    for name in _NAMES:
        a = np.ascontiguousarray(inputs[name])
        arrays[f"in_{name}"] = a
        args.append(nc.dram_tensor(f"in_{name}", a.shape, mybir.dt.from_np(a.dtype), kind="ExternalInput").ap())
    shape = arrays["in_L0_attn_x"].shape
    args.append(nc.dram_tensor("out_y", shape, F32, kind="ExternalOutput").ap())
    build(nc, *args)
    result = run_bass_kernel_spmd(nc, [arrays], core_ids=[0])
    return result.results[0]["out_y"]
```
